# Optimizing a Trainium2 kernel written in Bass

```python
import numpy as np
import jax
import jax.numpy as jnp

def _softmax(x, axis=-1):
    return jax.nn.softmax(x, axis=axis)

def _gelu(x):
    return jax.nn.gelu(x, approximate=True)

def _silu(x):
    return jax.nn.silu(x)

def _sigmoid(x):
    return jax.nn.sigmoid(x)

def _layernorm(x, axis=-1, eps=1e-05):
    m = jnp.mean(x, axis=axis, keepdims=True)
    v = jnp.var(x, axis=axis, keepdims=True)
    return (x - m) / jnp.sqrt(v + eps)

def _scatter_add(tgt, idx, src, axis=0):
    return tgt.at[idx].add(src)

def _segment_sum(src, seg, n):
    return jax.ops.segment_sum(src, seg, n)
kernel_name = 'mk_adj_ffn_d2_adj_r2_bc0423'

def setup_inputs(seed: int=0):
    np.random.seed(seed)
    _w = jnp.asarray

    def _rec_inputs():
        import jax
        import jax.numpy as jnp
        _gk = jax.random.key(seed)
        x = -0.0002928 + 1 * jax.random.normal(jax.random.fold_in(_gk, 1), (128, 128, 128), jnp.float32)
        _a = jax.random.bernoulli(jax.random.fold_in(_gk, 2), 0.0625, (128, 128, 128))
        _a = jnp.logical_or(_a, jnp.swapaxes(_a, -1, -2))
        _a = jnp.logical_or(_a, jnp.eye(128, dtype=bool))
        _af = _a.astype(jnp.float32)
        _af = _af * jax.random.uniform(jax.random.fold_in(_gk, 3), (128, 128, 128), jnp.float32, 0.05, 1)
        adj = _af
        return (x, adj)
    x, adj = _rec_inputs()

    def _L0_gnn_setup():
        import jax, jax.numpy as jnp
        import numpy as np
        B, N, D, H = (8, 1024, 128, 512)
        RMS_EPS = 1e-06

        def _rmsnorm(h, w, eps=RMS_EPS):
            var = jnp.mean(jnp.square(h), axis=-1, keepdims=True)
            return h * jax.lax.rsqrt(var + eps) * w
        key = jax.random.key(seed)
        ks = jax.random.split(key, 5)
        x = jax.random.normal(ks[0], (B, N, D), dtype=jnp.float32)
        adjacency = jax.random.uniform(ks[1], (B, N, N), dtype=jnp.float32)
        epsilon = jnp.zeros((), dtype=jnp.float32)
        W1 = jax.random.normal(ks[2], (D, H), dtype=jnp.float32) * (1.0 / np.sqrt(D))
        b1 = jnp.zeros((H,), dtype=jnp.float32)
        rms_weight = jnp.ones((H,), dtype=jnp.float32)
        W2 = jax.random.normal(ks[3], (H, D), dtype=jnp.float32) * (1.0 / np.sqrt(H))
        b2 = jnp.zeros((D,), dtype=jnp.float32)
        return {'x': x, 'adjacency': adjacency, 'epsilon': epsilon, 'W1': W1, 'b1': b1, 'rms_weight': rms_weight, 'W2': W2, 'b2': b2}
    _L0_gnn_all = _L0_gnn_setup()
    _L0_gnn_in = {k: v for k, v in _L0_gnn_all.items() if k in ('epsilon', 'W1', 'b1', 'rms_weight', 'W2', 'b2')}
    del _L0_gnn_all

    def _L0_ffn_setup():
        import jax, jax.numpy as jnp
        import numpy as np
        B, N, D = (16, 2048, 128)
        NUM_EXPERTS, TOP_K, HEADS = (4, 2, 4)
        N_EDGES = 524288
        LN_EPS = 1e-05

        def _layernorm(x, g, b):
            mu = x.mean(-1, keepdims=True)
            var = ((x - mu) ** 2).mean(-1, keepdims=True)
            return (x - mu) * jax.lax.rsqrt(var + LN_EPS) * g + b

        def _forward(x, edge_index, W_gat, att_src, att_dst, b_gat, ln_gamma, ln_beta, W1, b1, W2, b2):
            Bc, Nc, Dc = x.shape
            M = Bc * Nc
            x_flat = x.reshape(M, Dc)
            h = (x_flat @ W_gat).reshape(M, HEADS, NUM_EXPERTS)
            loops = jnp.arange(M, dtype=edge_index.dtype)
            src = jnp.concatenate([edge_index[0], loops])
            dst = jnp.concatenate([edge_index[1], loops])
            a_src = (h * att_src).sum(-1)
            a_dst = (h * att_dst).sum(-1)
            e = jax.nn.leaky_relu(a_src[src] + a_dst[dst], negative_slope=0.2)
            e_max = jax.ops.segment_max(e, dst, num_segments=M)
            ee = jnp.exp(e - e_max[dst])
            denom = jax.ops.segment_sum(ee, dst, num_segments=M)
            alpha = ee / (denom[dst] + 1e-16)
            msg = h[src] * alpha[:, :, None]
            agg = jax.ops.segment_sum(msg, dst, num_segments=M).reshape(M, HEADS * NUM_EXPERTS) + b_gat
            scores = _layernorm(agg, ln_gamma, ln_beta).reshape(M, HEADS, NUM_EXPERTS).mean(1)
            scores = scores.reshape(Bc, Nc, NUM_EXPERTS)
            topk_s, topk_i = jax.lax.top_k(scores, TOP_K)
            w = jax.nn.softmax(topk_s, axis=-1)
            out = jnp.zeros_like(x)
            for ei in range(NUM_EXPERTS):
                g = jnp.where(topk_i == ei, w, 0.0).sum(-1)
                hh = jax.nn.gelu(x @ W1[ei] + b1[ei], approximate=False)
                out = out + g[..., None] * (hh @ W2[ei] + b2[ei])
            return out
        key = jax.random.key(seed)
        ks = jax.random.split(key, 8)
        s = 0.05
        return {'x': jax.random.normal(ks[0], (B, N, D), jnp.float32), 'W_gat': jax.random.normal(ks[1], (D, HEADS * NUM_EXPERTS), jnp.float32) * s, 'att_src': jax.random.normal(ks[2], (HEADS, NUM_EXPERTS), jnp.float32) * s, 'att_dst': jax.random.normal(ks[3], (HEADS, NUM_EXPERTS), jnp.float32) * s, 'b_gat': jnp.zeros((HEADS * NUM_EXPERTS,), jnp.float32), 'ln_gamma': jnp.ones((HEADS * NUM_EXPERTS,), jnp.float32), 'ln_beta': jnp.zeros((HEADS * NUM_EXPERTS,), jnp.float32), 'W1': jax.random.normal(ks[4], (NUM_EXPERTS, D, 2 * D), jnp.float32) * s, 'b1': jnp.zeros((NUM_EXPERTS, 2 * D), jnp.float32), 'W2': jax.random.normal(ks[5], (NUM_EXPERTS, 2 * D, D), jnp.float32) * s, 'b2': jnp.zeros((NUM_EXPERTS, D), jnp.float32), 'edge_index': jax.random.randint(ks[6], (2, N_EDGES), 0, B * N, jnp.int32)}
    _L0_ffn_all = _L0_ffn_setup()
    _L0_ffn_in = {k: v for k, v in _L0_ffn_all.items() if k in ('W_gat', 'att_src', 'att_dst', 'b_gat', 'ln_gamma', 'ln_beta', 'W1', 'b1', 'W2', 'b2', 'edge_index')}
    del _L0_ffn_all

    def _L1_gnn_setup():
        import jax, jax.numpy as jnp
        import numpy as np
        ALPHA = 0.2
        NEG = -9000000000000000.0
        key = jax.random.key(seed)
        k1, k2, k3, k4 = jax.random.split(key, 4)
        B, N, F_in, F_out = (8, 1024, 128, 128)
        x = jax.random.normal(k1, (B, N, F_in), dtype=jnp.float32)
        adj = (jax.random.uniform(k2, (B, N, N)) < 0.05).astype(jnp.float32)
        W = jax.random.normal(k3, (F_in, F_out), jnp.float32) * (1.414 * np.sqrt(2.0 / (F_in + F_out)))
        a = jax.random.normal(k4, (2 * F_out, 1), jnp.float32) * (1.414 * np.sqrt(2.0 / (2 * F_out + 1)))
        return {'input': x, 'adj': adj, 'W': W, 'a': a}
    _L1_gnn_all = _L1_gnn_setup()
    _L1_gnn_in = {k: v for k, v in _L1_gnn_all.items() if k in ('W', 'a')}
    del _L1_gnn_all

    def _L1_ffn_setup():
        import jax, jax.numpy as jnp
        import numpy as np
        B, T, D, H, E = (16, 2048, 128, 256, 8)
        key = jax.random.key(seed)
        ks = jax.random.split(key, 5)
        x = jax.random.normal(ks[0], (B, T, D), dtype=jnp.float32)
        gate_w = jax.random.normal(ks[1], (D, E), dtype=jnp.float32) * 0.02
        gate_b = jnp.zeros((E,), dtype=jnp.float32)
        W1 = jax.random.normal(ks[2], (E, D, H), dtype=jnp.float32) * 0.02
        b1 = jnp.zeros((E, H), dtype=jnp.float32)
        W2 = jax.random.normal(ks[3], (E, H, D), dtype=jnp.float32) * 0.02
        b2 = jnp.zeros((E, D), dtype=jnp.float32)
        return {'x': x, 'gate_w': gate_w, 'gate_b': gate_b, 'W1': W1, 'b1': b1, 'W2': W2, 'b2': b2}
    _L1_ffn_all = _L1_ffn_setup()
    _L1_ffn_in = {k: v for k, v in _L1_ffn_all.items() if k in ('gate_w', 'gate_b', 'W1', 'b1', 'W2', 'b2')}
    del _L1_ffn_all
    return {'x': x, 'adj': adj, 'L0_gnn_epsilon': _L0_gnn_in['epsilon'], 'L0_gnn_W1': _L0_gnn_in['W1'], 'L0_gnn_b1': _L0_gnn_in['b1'], 'L0_gnn_rms_weight': _L0_gnn_in['rms_weight'], 'L0_gnn_W2': _L0_gnn_in['W2'], 'L0_gnn_b2': _L0_gnn_in['b2'], 'L0_ffn_W_gat': _L0_ffn_in['W_gat'], 'L0_ffn_att_src': _L0_ffn_in['att_src'], 'L0_ffn_att_dst': _L0_ffn_in['att_dst'], 'L0_ffn_b_gat': _L0_ffn_in['b_gat'], 'L0_ffn_ln_gamma': _L0_ffn_in['ln_gamma'], 'L0_ffn_ln_beta': _L0_ffn_in['ln_beta'], 'L0_ffn_W1': _L0_ffn_in['W1'], 'L0_ffn_b1': _L0_ffn_in['b1'], 'L0_ffn_W2': _L0_ffn_in['W2'], 'L0_ffn_b2': _L0_ffn_in['b2'], 'L0_ffn_edge_index': _L0_ffn_in['edge_index'], 'L1_gnn_W': _L1_gnn_in['W'], 'L1_gnn_a': _L1_gnn_in['a'], 'L1_ffn_gate_w': _L1_ffn_in['gate_w'], 'L1_ffn_gate_b': _L1_ffn_in['gate_b'], 'L1_ffn_W1': _L1_ffn_in['W1'], 'L1_ffn_b1': _L1_ffn_in['b1'], 'L1_ffn_W2': _L1_ffn_in['W2'], 'L1_ffn_b2': _L1_ffn_in['b2']}

def reference(x, adj, L0_gnn_epsilon, L0_gnn_W1, L0_gnn_b1, L0_gnn_rms_weight, L0_gnn_W2, L0_gnn_b2, L0_ffn_W_gat, L0_ffn_att_src, L0_ffn_att_dst, L0_ffn_b_gat, L0_ffn_ln_gamma, L0_ffn_ln_beta, L0_ffn_W1, L0_ffn_b1, L0_ffn_W2, L0_ffn_b2, L0_ffn_edge_index, L1_gnn_W, L1_gnn_a, L1_ffn_gate_w, L1_ffn_gate_b, L1_ffn_W1, L1_ffn_b1, L1_ffn_W2, L1_ffn_b2):
    import jax
    import jax.numpy as jnp

    def _L0_gnn_ref(x, adjacency, epsilon, W1, b1, rms_weight, W2, b2):
        import jax, jax.numpy as jnp
        import numpy as np
        B, N, D, H = (8, 1024, 128, 512)
        RMS_EPS = 1e-06

        def _rmsnorm(h, w, eps=RMS_EPS):
            var = jnp.mean(jnp.square(h), axis=-1, keepdims=True)
            return h * jax.lax.rsqrt(var + eps) * w
        neighbor_sum = jnp.einsum('bnm,bmd->bnd', adjacency, x)
        agg = epsilon * x + neighbor_sum
        h = jnp.einsum('bnd,dh->bnh', agg, W1) + b1
        h = jax.nn.silu(_rmsnorm(h, rms_weight))
        out = jnp.einsum('bnh,hd->bnd', h, W2) + b2
        return out

    def _L0_ffn_ref(x, W_gat, att_src, att_dst, b_gat, ln_gamma, ln_beta, W1, b1, W2, b2, edge_index):
        import jax, jax.numpy as jnp
        import numpy as np
        B, N, D = (16, 2048, 128)
        NUM_EXPERTS, TOP_K, HEADS = (4, 2, 4)
        N_EDGES = 524288
        LN_EPS = 1e-05

        def _layernorm(x, g, b):
            mu = x.mean(-1, keepdims=True)
            var = ((x - mu) ** 2).mean(-1, keepdims=True)
            return (x - mu) * jax.lax.rsqrt(var + LN_EPS) * g + b

        def _forward(x, edge_index, W_gat, att_src, att_dst, b_gat, ln_gamma, ln_beta, W1, b1, W2, b2):
            Bc, Nc, Dc = x.shape
            M = Bc * Nc
            x_flat = x.reshape(M, Dc)
            h = (x_flat @ W_gat).reshape(M, HEADS, NUM_EXPERTS)
            loops = jnp.arange(M, dtype=edge_index.dtype)
            src = jnp.concatenate([edge_index[0], loops])
            dst = jnp.concatenate([edge_index[1], loops])
            a_src = (h * att_src).sum(-1)
            a_dst = (h * att_dst).sum(-1)
            e = jax.nn.leaky_relu(a_src[src] + a_dst[dst], negative_slope=0.2)
            e_max = jax.ops.segment_max(e, dst, num_segments=M)
            ee = jnp.exp(e - e_max[dst])
            denom = jax.ops.segment_sum(ee, dst, num_segments=M)
            alpha = ee / (denom[dst] + 1e-16)
            msg = h[src] * alpha[:, :, None]
            agg = jax.ops.segment_sum(msg, dst, num_segments=M).reshape(M, HEADS * NUM_EXPERTS) + b_gat
            scores = _layernorm(agg, ln_gamma, ln_beta).reshape(M, HEADS, NUM_EXPERTS).mean(1)
            scores = scores.reshape(Bc, Nc, NUM_EXPERTS)
            topk_s, topk_i = jax.lax.top_k(scores, TOP_K)
            w = jax.nn.softmax(topk_s, axis=-1)
            out = jnp.zeros_like(x)
            for ei in range(NUM_EXPERTS):
                g = jnp.where(topk_i == ei, w, 0.0).sum(-1)
                hh = jax.nn.gelu(x @ W1[ei] + b1[ei], approximate=False)
                out = out + g[..., None] * (hh @ W2[ei] + b2[ei])
            return out
        return _forward(x, edge_index, W_gat, att_src, att_dst, b_gat, ln_gamma, ln_beta, W1, b1, W2, b2)

    def _L1_gnn_ref(input, adj, W, a):
        import jax, jax.numpy as jnp
        import numpy as np
        ALPHA = 0.2
        NEG = -9000000000000000.0
        F_out = W.shape[1]
        h = input @ W
        a1 = a[:F_out, 0]
        a2 = a[F_out:, 0]
        s = jnp.einsum('bnf,f->bn', h, a1 + a2)
        e = jax.nn.leaky_relu(s, ALPHA)[:, :, None]
        logits = jnp.where(adj > 0, e, NEG)
        att = jax.nn.softmax(logits, axis=2)
        h_prime = jnp.einsum('bij,bjf->bif', att, h)
        return jax.nn.elu(h_prime)

    def _L1_ffn_ref(x, gate_w, gate_b, W1, b1, W2, b2):
        import jax, jax.numpy as jnp
        import numpy as np
        B, T, D, H, E = (16, 2048, 128, 256, 8)
        Bb, Tt, Dd = x.shape
        Ee = gate_w.shape[1]
        xf = x.reshape(-1, Dd)
        N = xf.shape[0]
        logits = xf @ gate_w + gate_b
        probs = jax.nn.softmax(logits, axis=-1)
        top2_vals, top2_idx = jax.lax.top_k(probs, 2)
        cw = jnp.zeros((N, Ee), dtype=xf.dtype).at[jnp.arange(N)[:, None], top2_idx].add(top2_vals)

        def step(acc, params):
            w1, bb1, w2, bb2, we = params
            h = jax.nn.gelu(xf @ w1 + bb1, approximate=False)
            y = h @ w2 + bb2
            return (acc + we[:, None] * y, None)
        out, _ = jax.lax.scan(step, jnp.zeros_like(xf), (W1, b1, W2, b2, cw.T))
        return out.reshape(Bb, Tt, Dd)
    x = x + _L0_gnn_ref(_layernorm(x, axis=-1), adj, L0_gnn_epsilon, L0_gnn_W1, L0_gnn_b1, L0_gnn_rms_weight, L0_gnn_W2, L0_gnn_b2)
    x = x + _L0_ffn_ref(_layernorm(x, axis=-1), L0_ffn_W_gat, L0_ffn_att_src, L0_ffn_att_dst, L0_ffn_b_gat, L0_ffn_ln_gamma, L0_ffn_ln_beta, L0_ffn_W1, L0_ffn_b1, L0_ffn_W2, L0_ffn_b2, L0_ffn_edge_index)
    x = x + _L1_gnn_ref(_layernorm(x, axis=-1), adj, L1_gnn_W, L1_gnn_a)
    x = x + _L1_ffn_ref(_layernorm(x, axis=-1), L1_ffn_gate_w, L1_ffn_gate_b, L1_ffn_W1, L1_ffn_b1, L1_ffn_W2, L1_ffn_b2)
    return x

_drawn_inputs = setup_inputs


def setup_inputs(seed=0):
    import zlib

    import numpy as np

    out = dict(_drawn_inputs(seed))
    spreads = {'L0_gnn_b1': (0.0, 0.1),
     'L0_gnn_rms_weight': (1.0, 0.2),
     'L0_gnn_b2': (0.0, 0.1),
     'L0_ffn_b_gat': (0.0, 0.1),
     'L0_ffn_ln_gamma': (1.0, 0.2),
     'L0_ffn_ln_beta': (0.0, 0.1),
     'L0_ffn_b1': (0.0, 0.1),
     'L0_ffn_b2': (0.0, 0.1),
     'L1_ffn_gate_b': (0.0, 0.8),
     'L1_ffn_b1': (0.0, 0.8),
     'L1_ffn_b2': (0.0, 0.428)}
    factors = {'L0_ffn_att_src': 3.162,
     'L0_ffn_att_dst': 4.872,
     'L1_ffn_gate_w': 3.323,
     'L1_ffn_W1': 8.0,
     'L1_ffn_W2': 7.371}
    for name, (base, spread) in spreads.items():
        noise = np.random.default_rng([zlib.crc32(name.encode()), seed]).standard_normal(out[name].shape)
        drawn = base * np.exp(spread * noise) if base else spread * noise
        out[name] = jnp.asarray(drawn.astype(out[name].dtype))
    for name, factor in factors.items():
        out[name] = (out[name] * factor).astype(out[name].dtype)
    return out
```

```python
from contextlib import ExitStack

import concourse.bass as bass
from concourse import mybir

F32 = mybir.dt.float32
U32 = mybir.dt.uint32
I32 = mybir.dt.int32
BF16 = mybir.dt.bfloat16
ALU = mybir.AluOpType
ACT = mybir.ActivationFunctionType
AX = mybir.AxisListType

P = 128
LN_EPS = 1e-05
RMS_EPS = 1e-06
NEG = -9000000000000000.0
SLOPE = 0.2
TB = 4

HEADS = 4
CH = 4
HC = HEADS * CH
ROW = HC + HEADS

STREAMS = 8
HALF = 2
CHUNKS = HALF * STREAMS
BK = 4
GROUP = 512
GC = GROUP // P


class Scope:

    def __init__(self, nc, tag):
        self.nc, self.tag, self.ctx = nc, tag, ExitStack()

    def __enter__(self):
        return self

    def __exit__(self, *a):
        return self.ctx.__exit__(*a)

    def sb(self, name, shape, dt=F32):
        return self.ctx.enter_context(self.nc.sbuf_tensor(f"{self.tag}_{name}", shape, dt))

    def bank(self, name):
        return self.ctx.enter_context(self.nc.psum_tensor(f"{self.tag}_{name}", [P, 512], F32))

    def sem(self, name):
        return self.ctx.enter_context(self.nc.semaphore(f"{self.tag}_{name}"))

    def block(self):
        return self.ctx.enter_context(self.nc.Block())


class Done:

    def __init__(self, eng, sem):
        self.eng, self.sem, self.base, self.n = eng, sem, 0, 0

    def link(self, ins):
        self.n += 1
        ins.then_inc(self.sem, 1)
        self.eng.wait_ge(self.sem, self.base + self.n)

    def mark(self, ins):
        self.n += 1
        ins.then_inc(self.sem, 1)

    def wait(self):
        self.eng.wait_ge(self.sem, self.base + self.n)


def rows_of(vector_ap, n):
    return vector_ap.rearrange("(a n) -> a n", a=1).broadcast_to([P, n])


def flat(ap):
    return ap.rearrange("p a b -> p (a b)")


def over(ap, shape):
    return ap.broadcast_to(shape)


def sort_edges(nc, edge_index, sorted_edges, groups_keep, nodes):
    n_edges = edge_index.shape[1]
    cols = n_edges // P
    scols = cols // STREAMS
    iters = scols // (2 * HALF)
    blocks = nodes // P
    gmax = n_edges // GROUP + blocks
    slots = sorted_edges.shape[0]
    mark_value = nodes * P
    shift = GROUP.bit_length() - 1

    with Scope(nc, "sort") as s:
        target = s.sb("target", [P, cols], I32)
        packed = s.sb("packed", [P, cols], I32)
        block_of = s.sb("block_of", [P, cols])
        empty = s.sb("empty", [P, slots // P // 8], I32)
        iota_f = s.sb("iota_f", [P, P])
        iota_b = s.sb("iota_b", [P, P], BF16)
        before = s.sb("before", [P, P], BF16)
        notbefore = s.sb("notbefore", [P, P], BF16)
        ones_b = s.sb("ones_b", [P, P], BF16)
        ones_f = s.sb("ones_f", [P, P])
        zeros_b = s.sb("zeros_b", [P, 512], BF16)
        zeros = s.sb("zeros", [P, P])
        onehot = s.sb("onehot", [P, 2, HALF, STREAMS, P], BF16)
        keycol = s.sb("keycol", [P, 2, CHUNKS])
        slot_f = s.sb("slot_f", [P, 2, CHUNKS])
        dropped = s.sb("dropped", [P, 2, CHUNKS])
        slot_i = s.sb("slot_i", [P, 2, CHUNKS], I32)
        value = s.sb("value", [P, 2, CHUNKS], I32)
        scrap = s.sb("scrap", [P, CHUNKS, P], BF16)
        count = s.sb("count", [P, STREAMS, P])
        total = s.sb("total", [P, P])
        whole = s.sb("whole", [P, P], I32)
        block_end = s.sb("block_end", [P, P])
        start = s.sb("start", [P, STREAMS, P])
        group_iota = s.sb("group_iota", [P, gmax])
        past_end = s.sb("past_end", [P, gmax])
        end_col = s.sb("end_col", [P, 1])
        ranks = [s.bank(f"ranks{k}") for k in range(2)]
        sums = [s.bank(f"sums{k}") for k in range(3)]
        col = s.bank("col")

        loaded = s.sem("loaded")
        filled = s.sem("filled")
        consts = s.sem("consts")
        own = s.sem("own")
        onehot_ready = s.sem("onehot_ready")
        onehot_counted = s.sem("onehot_counted")
        start_ready = s.sem("start_ready")
        end_turned = s.sem("end_turned")
        past_ready = s.sem("past_ready")
        groups_summed = s.sem("groups_summed")
        ranked = s.sem("ranked")
        extracted = s.sem("extracted")
        slots_ready = s.sem("slots_ready")
        turn = s.sem("turn")
        scattered = [s.sem(f"scattered{h}") for h in range(2)]
        block = s.block()

        edges = edge_index.rearrange("t (p c) -> t p c", p=P)

        def bank_of(h, step, k):
            return onehot[:, h, step, BK * k:BK * k + BK, :].rearrange("p a b -> p (a b)")

        @block.sync
        def _(sp):
            sp.dma_start(packed[:, :], edges[0]).then_inc(loaded, 16)
            sp.dma_start(target[:, :], edges[1]).then_inc(loaded, 16)
            sp.wait_ge(consts, 1)
            view = sorted_edges.rearrange("(k p c) o -> k p (c o)", k=8, p=P)
            for k in range(8):
                sp.dma_start(view[k], empty[:, :]).then_inc(filled, 16)
            sp.wait_ge(filled, 8 * 16)

        @block.gpsimd
        def _(pool):
            pool.memset(empty[:, :], mark_value).then_inc(consts, 1)
            pool.iota(iota_f[:, :], [[1, P]], base=0, channel_multiplier=0,
                      allow_small_or_imprecise_dtypes=True).then_inc(consts, 1)
            pool.iota(group_iota[:, :], [[1, gmax]], base=0, channel_multiplier=0,
                      allow_small_or_imprecise_dtypes=True).then_inc(consts, 1)
            pool.memset(ones_b[:, :], 1.0).then_inc(consts, 1)
            pool.memset(ones_f[:, :], 1.0).then_inc(consts, 1)
            pool.memset(zeros[:, :], 0.0).then_inc(consts, 1)
            pool.memset(zeros_b[:, :], 0.0).then_inc(consts, 1)
            pool.wait_ge(consts, 7)
            pool.affine_select(out=before[:, :], in_=ones_b[:, :], compare_op=ALU.is_gt, fill=0.0, base=0,
                               pattern=[[1, P]], channel_multiplier=-1).then_inc(consts, 1)
            pool.affine_select(out=notbefore[:, :], in_=ones_b[:, :], compare_op=ALU.is_ge, fill=0.0, base=0,
                               pattern=[[-1, P]], channel_multiplier=1).then_inc(consts, 1)
            pool.wait_ge(filled, 8 * 16)
            last_slot = pool.to_reg(slots - 1)
            with pool.Fori(0, iters) as i:
                for h in range(2):
                    pool.wait_ge(slots_ready, 4 * i + 2 * h + 2)
                    pool.sem_inc(turn, 1)
                    for k in range(CHUNKS):
                        pool.indirect_dma_start(
                            out=sorted_edges,
                            out_offset=bass.IndirectOffsetOnAxis(ap=slot_i[:, h, k:k + 1].bitcast(U32), axis=0),
                            in_=value[:, h, k:k + 1], in_offset=None,
                            bounds_check=last_slot, oob_is_err=False).then_inc(scattered[h], 16)
            for h in range(2):
                pool.wait_ge(scattered[h], iters * CHUNKS * 16)

        @block.tensor
        def _(pe):
            pe.wait_ge(consts, 9)
            for k in range(2):
                pe.matmul(ranks[k][:, :], ones_b[:, :], zeros_b[:, :], start=True, stop=False,
                          skip_group_check=True)
            with pe.Fori(0, iters) as i:
                for h in range(2):
                    pe.wait_ge(onehot_ready, 2 * i + h + 1)
                    for step in range(HALF):
                        for k in range(2):
                            mm = pe.matmul(ranks[k][:, :], ones_b[:, :], bank_of(h, step, k),
                                           start=False, stop=False, skip_group_check=True)
                    mm.then_inc(onehot_counted, 1)
            pe.wait_ge(start_ready, 1)
            pe.matmul(col[:, 0:1], block_end[0:1, :], ones_f[0:1, 0:1], start=True, stop=True)\
                .then_inc(end_turned, 1)
            for k in range(2):
                pe.matmul(ranks[k][:, :], ones_f[0:1, :],
                          start[0:1, BK * k:BK * k + BK, :].rearrange("p a b -> p (a b)"),
                          start=True, stop=False, skip_group_check=True)
            pe.wait_ge(past_ready, 1)
            for k in range(3):
                w = min(512, gmax - 512 * k)
                mm = pe.matmul(sums[k][:, 0:w], ones_f[:, :], past_end[:, 512 * k:512 * k + w],
                               start=True, stop=True)
            mm.then_inc(groups_summed, 1)
            with pe.Fori(0, iters) as i:
                for h in range(2):
                    pe.wait_ge(onehot_ready, 2 * iters + 2 * i + h + 1)
                    for step in range(HALF):
                        for k in range(2):
                            n = (h * HALF + step) * 2 + k
                            if n > 1:
                                pe.wait_ge(extracted, i * 8 + n - 1)
                                pe.matmul(ranks[k][:, :], notbefore[:, :],
                                          bank_of(h if step else 1 - h, (step - 1) % HALF, k),
                                          start=False, stop=False, skip_group_check=True)
                            pe.matmul(ranks[k][:, :], before[:, :], bank_of(h, step, k),
                                      start=False, stop=False, skip_group_check=True).then_inc(ranked, 1)
                for k in range(2):
                    pe.wait_ge(extracted, i * 8 + 7 + k)
                    pe.matmul(ranks[k][:, :], notbefore[:, :], bank_of(1, HALF - 1, k),
                              start=False, stop=False, skip_group_check=True)

        @block.vector
        def _(v):
            me = Done(v, own)
            v.wait_ge(loaded, 32)
            v.wait_ge(consts, 9)
            v.tensor_copy(iota_b[:, :], iota_f[:, :])
            v.tensor_single_scalar(packed[:, :], packed[:, :], nodes - 1, ALU.min)
            low = block_of[:, :].bitcast(I32)
            me.link(v.tensor_single_scalar(low, target[:, :], P - 1, ALU.bitwise_and))
            me.link(v.scalar_tensor_tensor(out=packed[:, :], in0=packed[:, :], scalar=float(P), in1=low,
                                           op0=ALU.mult, op1=ALU.add))
            me.link(v.tensor_single_scalar(target[:, :], target[:, :], 7, ALU.logical_shift_right))
            me.link(v.tensor_copy(block_of[:, :], target[:, :]))
            keys = block_of[:, :].rearrange("p (s c) -> p c s", s=STREAMS)
            values = packed[:, :].rearrange("p (s c) -> p c s", s=STREAMS)

            def build(c, h):
                me.link(v.tensor_copy(keycol[:, h, :].rearrange("p (a b) -> p a b", a=HALF),
                                      keys[:, bass.ds(c, HALF), :]))
                for t in range(CHUNKS):
                    ins = v.tensor_scalar(onehot[:, h, t // STREAMS, t % STREAMS, :], iota_b[:, :],
                                          keycol[:, h, t:t + 1], None, ALU.is_equal)
                ins.then_inc(onehot_ready, 1)

            for h in range(2):
                build(h * HALF, h)
            first = me.n
            with v.Fori(1, iters) as i:
                me.base, me.n = first + (i - 1) * 2, 0
                for h in range(2):
                    v.wait_ge(onehot_counted, 2 * i + h - 1)
                    build((2 * i + h) * HALF, h)
            me.base, me.n = 0, first + (iters - 1) * 2
            v.wait_ge(onehot_counted, 2 * iters)
            for k in range(2):
                me.link(v.tensor_copy(count[:, BK * k:BK * k + BK, :].rearrange("p a b -> p (a b)"),
                                      ranks[k][:, :]))
            me.link(v.tensor_reduce(total[:, :], count[:, :, :].rearrange("p s b -> p b s"), AX.X, ALU.add))
            me.link(v.tensor_scalar(total[:, :], total[:, :], float(GROUP - 1), None, ALU.add))
            me.link(v.tensor_copy(whole[:, :], total[:, :]))
            me.link(v.tensor_scalar(whole[:, :], whole[:, :], shift, shift, ALU.logical_shift_right,
                                    ALU.logical_shift_left))
            me.link(v.tensor_copy(total[:, :], whole[:, :]))
            me.link(v.tensor_tensor_scan(block_end[:, :], zeros[:, :], total[:, :], 0.0, ALU.add, ALU.add))
            me.link(v.tensor_tensor(start[:, 0, :], block_end[:, :], total[:, :], ALU.subtract))
            for t in range(1, STREAMS):
                ins = v.tensor_tensor(start[:, t, :], start[:, t - 1, :], count[:, t - 1, :], ALU.add)
                if t < STREAMS - 1:
                    me.link(ins)
            ins.then_inc(start_ready, 1)
            v.wait_ge(end_turned, 1)
            me.link(v.tensor_scalar(end_col[:, :], col[:, 0:1], 1.0 / GROUP, None, ALU.mult))
            v.tensor_scalar(past_end[:, :], group_iota[:, :], end_col[:, 0:1], None, ALU.is_ge)\
                .then_inc(past_ready, 1)
            v.wait_ge(groups_summed, 1)
            for k in range(3):
                w = min(512, gmax - 512 * k)
                v.tensor_scalar(groups_keep[:, 512 * k:512 * k + w], sums[k][:, 0:w], float(P - 1), None,
                                ALU.min)
            me.link(v.tensor_scalar(whole[:, 0:1], block_end[:, P - 1:P], 1.0 / GROUP, 1.0, ALU.mult, ALU.add))
            me.link(v.tensor_single_scalar(whole[:, 0:1], whole[:, 0:1], 1, ALU.logical_shift_right))
            me.link(v.tensor_single_scalar(groups_keep[:, gmax:gmax + 1], whole[:, 0:1], 1, ALU.max))

            second = me.n

            def slots_of(i, h, first_use):
                build((2 * i + h) * HALF, h)
                for step in range(HALF):
                    for k in range(2):
                        n = (h * HALF + step) * 2 + k
                        v.wait_ge(ranked, i * 8 + n + 1)
                        for q in range(BK):
                            t = step * STREAMS + BK * k + q
                            ins = v.tensor_tensor_reduce(
                                out=scrap[:, t, :], in0=ranks[k][:, P * q:P * q + P],
                                in1=onehot[:, h, step, BK * k + q, :], scale=1.0, scalar=0.0,
                                op0=ALU.mult, op1=ALU.add, accum_out=slot_f[:, h, t:t + 1])
                        ins.then_inc(extracted, 1)
                me.link(v.tensor_scalar(dropped[:, h, :], keycol[:, h, :], float(blocks), float(1 << 22),
                                        ALU.is_ge, ALU.mult))
                v.wait_ge(extracted, i * 8 + (h + 1) * 4)
                if not first_use:
                    v.wait_ge(scattered[h], i * (CHUNKS * 16))
                v.tensor_tensor(slot_i[:, h, :], slot_f[:, h, :], dropped[:, h, :], ALU.add)\
                    .then_inc(slots_ready, 1)
                v.tensor_copy(value[:, h, :].rearrange("p (a b) -> p a b", a=HALF),
                              values[:, bass.ds((2 * i + h) * HALF, HALF), :]).then_inc(slots_ready, 1)

            for h in range(2):
                slots_of(0, h, True)
            assert me.n == second + 4
            with v.Fori(1, iters) as i:
                me.base, me.n = second + i * 4, 0
                for h in range(2):
                    slots_of(i, h, False)


def rsqrt(me, v, x, work, y):
    me.link(v.tensor_single_scalar(work.bitcast(I32), x.bitcast(I32), 1, ALU.logical_shift_right))
    me.link(v.tensor_scalar(y.bitcast(I32), work.bitcast(I32), -1.0, float(0x5F3759DF), ALU.mult, ALU.add))
    for _ in range(3):
        me.link(v.tensor_tensor(work, y, y, ALU.mult))
        me.link(v.scalar_tensor_tensor(out=work, in0=work, scalar=-0.5, in1=x, op0=ALU.mult, op1=ALU.mult))
        me.link(v.scalar_tensor_tensor(out=y, in0=work, scalar=1.5, in1=y, op0=ALU.add, op1=ALU.mult))


def norm_rows(v, me, turn, src, stats, mv, rstd, out):
    v.sem_inc(turn, 1)
    for j in range(TB):
        me.mark(v.bn_stats(stats[:, j, :], src[j]))
    me.wait()
    v.sem_inc(turn, 1)
    for j in range(TB):
        me.mark(v.bn_aggr(mv[:, j, 0:2], stats[:, j, :]))
    me.wait()
    me.link(v.tensor_scalar(mv[:, :, 2], mv[:, :, 1], LN_EPS, None, ALU.add))
    rsqrt(me, v, mv[:, :, 2], mv[:, :, 3], rstd[:, :])
    for j in range(TB):
        ins = v.tensor_scalar(out[:, j, :], src[j], mv[:, j, 0:1], rstd[:, j:j + 1], ALU.subtract, ALU.mult)
    return ins


def gin_layer(nc, x, adj, w, keep):
    tiles = x.shape[0]
    groups = tiles // TB
    H = w["W1"].shape[1]
    HK = H // P
    x_keep, xt_keep, proj_keep = keep["x"], keep["xt"], keep["h"]
    with Scope(nc, "gin") as s:
        ident = s.sb("ident", [P, P])
        adj_sb = s.sb("adj", [P, 2, TB, P])
        adj_t = s.sb("adj_t", [P, TB, P])
        xn = s.sb("xn", [P, TB, P])
        agg_t = s.sb("agg_t", [P, TB, P])
        hb = s.sb("hb", [P, 2, H])
        hs = s.sb("hs", [P, 2, H])
        sq = s.sb("sq", [P, H])
        ht = s.sb("ht", [P, 2, H])
        xt = s.sb("xt", [P, TB, P])
        stats = s.sb("stats", [P, TB, 6])
        mv = s.sb("mv", [P, TB, 4])
        rstd = s.sb("rstd", [P, TB])
        ss = s.sb("ss", [P, TB])
        rms = s.sb("rms", [P, TB])
        rin = s.sb("rin", [P, 2])
        eps_col = s.sb("eps_col", [P, 1])
        w1 = s.sb("w1", [P, H])
        w2 = s.sb("w2", [P, HK, P])
        b1 = s.sb("b1", [P, H])
        rw = s.sb("rw", [P, H])
        b2 = s.sb("b2", [P, P])
        wg = s.sb("wg", [P, HC])
        b_adj = s.bank("b_adj")
        b_agg = s.bank("b_agg")
        b_h = [s.bank(f"b_h{k}") for k in range(2)]
        b_ht = s.bank("b_ht")
        b_o = s.bank("b_o")
        b_xt = s.bank("b_xt")
        b_p = s.bank("b_p")

        weights = s.sem("weights")
        consts = s.sem("consts")
        own = s.sem("own")
        turn = s.sem("turn")
        arrived = [s.sem(f"arrived{k}") for k in range(2)]
        adj_turned = s.sem("adj_turned")
        adj_ready = s.sem("adj_ready")
        xn_ready = s.sem("xn_ready")
        agg_done = s.sem("agg_done")
        agg_ready = s.sem("agg_ready")
        h_done = s.sem("h_done")
        hb_ready = s.sem("hb_ready")
        squared = s.sem("squared")
        hn_ready = s.sem("hn_ready")
        silu_ready = s.sem("silu_ready")
        h_turned = s.sem("h_turned")
        ht_ready = s.sem("ht_ready")
        out_done = s.sem("out_done")
        norm_ready = s.sem("norm_ready")
        x_turned = s.sem("x_turned")
        xt_ready = s.sem("xt_ready")
        xt_kept = s.sem("xt_kept")
        proj_done = s.sem("proj_done")
        proj_kept = s.sem("proj_kept")
        block = s.block()

        xv = x.rearrange("t n d -> n t d")
        av = adj.rearrange("t n m -> n t m")
        PG = 2 * TB

        @block.sync
        def _(sp):
            for dst, src in ((w1[:, :], w["W1"]), (w2[:, :, :], w["W2"].rearrange("(k p) d -> p k d", p=P)),
                             (b1[:, :], rows_of(w["b1"], H)), (rw[:, :], rows_of(w["rms"], H)),
                             (b2[:, :], rows_of(w["b2"], P)), (wg[:, :], w["W_gat"]),
                             (eps_col[:, :], rows_of(w["eps"], 1))):
                sp.dma_start(dst, src).then_inc(weights, 16)

            def load(t0, k):
                sp.dma_start(adj_sb[:, k, :, :], av[:, bass.ds(t0, TB), :]).then_inc(arrived[k], 16)
                sp.dma_start(x_keep[:, bass.ds(t0, TB), :], xv[:, bass.ds(t0, TB), :]).then_inc(arrived[k], 16)

            for k in range(2):
                load(k * TB, k)
            with sp.Fori(0, groups // 2 - 1) as i:
                for k in range(2):
                    sp.wait_ge(adj_turned, 2 * i + k + 1)
                    load(PG * i + PG + k * TB, k)

        @block.gpsimd
        def _(pool):
            pool.memset(ident[:, :], 0.0).then_inc(consts, 1)
            pool.wait_ge(consts, 1)
            pool.affine_select(out=ident[:, :], in_=ident[:, :], compare_op=ALU.not_equal, fill=1.0,
                               base=0, pattern=[[-1, P]], channel_multiplier=1).then_inc(consts, 1)
            with pool.Fori(0, groups) as g:
                pool.wait_ge(xt_ready, g + 1)
                pool.tensor_copy(xt_keep[:, bass.ds(g * TB, TB), :], xt[:, :, :]).then_inc(xt_kept, 1)

        @block.tensor
        def _(pe):
            pe.wait_ge(weights, 16 * 7)
            pe.wait_ge(consts, 2)
            with pe.Fori(0, groups // 2) as i:
                for k in range(2):
                    g = 2 * i + k
                    pe.wait_ge(arrived[k], 32 * i + 32)
                    for j in range(TB):
                        mm = pe.transpose(b_adj[:, P * j:P * j + P], adj_sb[:, k, j, :], ident[:, :])
                    mm.then_inc(adj_turned, 1)
                    pe.wait_ge(adj_ready, g + 1)
                    pe.wait_ge(xn_ready, g + 1)
                    for j in range(TB):
                        mm = pe.matmul(b_agg[:, P * j:P * j + P], xn[:, j, :], adj_t[:, j, :],
                                       start=True, stop=True)
                    mm.then_inc(agg_done, 1)
                    pe.wait_ge(agg_ready, g + 1)

                    def hidden(j):
                        if j > 1:
                            pe.wait_ge(hb_ready, g * TB + j - 1)
                        pe.matmul(b_h[j % 2][:, :], agg_t[:, j, :], w1[:, :], start=True, stop=True)\
                            .then_inc(h_done, 1)

                    hidden(0)
                    for j in range(TB):
                        if j + 1 < TB:
                            hidden(j + 1)
                        pe.wait_ge(silu_ready, g * TB + j + 1)
                        if j:
                            pe.wait_ge(ht_ready, g * TB + j)
                        for c in range(HK):
                            mm = pe.transpose(b_ht[:, P * c:P * c + P], hs[:, j % 2, P * c:P * c + P],
                                              ident[:, :])
                        mm.then_inc(h_turned, 1)
                        pe.wait_ge(ht_ready, g * TB + j + 1)
                        for c in range(HK):
                            mm = pe.matmul(b_o[:, P * j:P * j + P], ht[:, j % 2, P * c:P * c + P], w2[:, c, :],
                                           start=(c == 0), stop=(c == HK - 1))
                    mm.then_inc(out_done, 1)
                    pe.wait_ge(norm_ready, g + 1)
                    for j in range(TB):
                        mm = pe.transpose(b_xt[:, P * j:P * j + P], xn[:, j, :], ident[:, :])
                    mm.then_inc(x_turned, 1)
                    pe.wait_ge(xt_ready, g + 1)
                    for j in range(TB):
                        mm = pe.matmul(b_p[:, HC * j:HC * j + HC], xt[:, j, :], wg[:, :], start=True, stop=True)
                    mm.then_inc(proj_done, 1)

        @block.scalar
        def _(act):
            act.wait_ge(weights, 16 * 7)
            with act.Fori(0, groups) as g:
                act.wait_ge(agg_done, g + 1)
                act.activation(flat(agg_t[:, :, :]), b_agg[:, :], ACT.Copy).then_inc(agg_ready, 1)
                for j in range(TB):
                    act.wait_ge(hb_ready, g * TB + j + 1)
                    act.activation(sq[:, :], hb[:, j % 2, :], ACT.Square, accum_out=ss[:, j:j + 1])\
                        .then_inc(squared, 1)
                    act.wait_ge(hn_ready, g * TB + j + 1)
                    act.activation(hs[:, j % 2, :], hb[:, j % 2, :], ACT.Silu).then_inc(silu_ready, 1)
                    act.wait_ge(h_turned, g * TB + j + 1)
                    act.activation(ht[:, j % 2, :], b_ht[:, :], ACT.Copy).then_inc(ht_ready, 1)
                act.wait_ge(x_turned, g + 1)
                act.wait_ge(xt_kept, g + 1)
                act.activation(flat(xt[:, :, :]), b_xt[:, :], ACT.Copy).then_inc(xt_ready, 1)

        @block.vector
        def _(v):
            me = Done(v, own)
            v.wait_ge(weights, 16 * 7)
            v.wait_ge(consts, 2)
            v.sem_inc(xt_kept, 1)
            per = 28+22+4*10
            with v.Fori(0, groups // 2) as i:
                for k in range(2):
                    g = 2 * i + k
                    me.base, me.n = per * g, 0
                    src = x_keep[:, bass.ds(g * TB, TB), :]
                    v.wait_ge(arrived[k], 32 * i + 32)
                    norm_rows(v, me, turn, [src[:, j, :] for j in range(TB)], stats, mv, rstd, xn).then_inc(xn_ready, 1)
                    v.wait_ge(adj_turned, g + 1)
                    v.scalar_tensor_tensor(
                        out=adj_t[:, :, :], in0=over(ident[:, :].unsqueeze(1), [P, TB, P]),
                        scalar=eps_col[:, 0:1], in1=b_adj[:, :].rearrange("p (a b) -> p a b", a=TB),
                        op0=ALU.mult, op1=ALU.add).then_inc(adj_ready, 1)

                    def bias(j):
                        v.wait_ge(h_done, g * TB + j + 1)
                        if j > 1:
                            v.wait_ge(silu_ready, g * TB + j - 1)
                        v.tensor_tensor(hb[:, j % 2, :], b_h[j % 2][:, :], b1[:, :], ALU.add).then_inc(hb_ready, 1)

                    bias(0)
                    for j in range(TB):
                        if j + 1 < TB:
                            bias(j + 1)
                        v.wait_ge(squared, g * TB + j + 1)
                        me.link(v.tensor_scalar(rin[:, 0:1], ss[:, j:j + 1], 1.0 / H, RMS_EPS, ALU.mult, ALU.add))
                        rsqrt(me, v, rin[:, 0:1], rin[:, 1:2], rms[:, j:j + 1])
                        v.scalar_tensor_tensor(out=hb[:, j % 2, :], in0=hb[:, j % 2, :], scalar=rms[:, j:j + 1],
                                               in1=rw[:, :], op0=ALU.mult, op1=ALU.mult).then_inc(hn_ready, 1)
                    me.link(v.tensor_tensor(src, src, over(b2[:, :].unsqueeze(1), [P, TB, P]), ALU.add))
                    v.wait_ge(out_done, g + 1)
                    me.link(v.tensor_tensor(src, src, b_o[:, :].rearrange("p (a b) -> p a b", a=TB), ALU.add))
                    norm_rows(v, me, turn, [src[:, j, :] for j in range(TB)], stats, mv, rstd, xn)\
                        .then_inc(norm_ready, 1)
                    v.wait_ge(proj_done, g + 1)
                    v.tensor_copy(proj_keep[:, bass.ds(g * TB, TB), 0:HC],
                                  b_p[:, 0:TB * HC].rearrange("p (a b) -> p a b", a=TB)).then_inc(proj_kept, 1)
                    n = me.n
            assert n == per, n


def edge_attention(nc, w, sorted_edges, table, keep):
    tiles = keep["x"].shape[1]
    nodes = tiles * P
    hk, dst_keep, acc, groups_keep, gates = keep["h"], keep["dst"], keep["acc"], keep["groups"], keep["gates"]
    gmax = groups_keep.shape[1] - 1
    E = CH
    with Scope(nc, "att") as s:
        ident = s.sb("ident", [P, P])
        iota_f = s.sb("iota_f", [P, P])
        att_src = s.sb("att_src", [P, HC])
        att_dst = s.sb("att_dst", [P, HC])
        b_gat = s.sb("b_gat", [P, HC])
        gamma = s.sb("gamma", [P, HC])
        beta = s.sb("beta", [P, HC])
        prod = s.sb("prod", [P, tiles, HC])
        self_e = s.sb("self_e", [P, tiles, HEADS])
        bound = s.sb("bound", [P, tiles, HEADS])
        small = s.sb("small", [P, tiles])
        small2 = s.sb("small2", [P, tiles])
        rs = s.sb("rs", [P, tiles])
        top = s.sb("top", [P, HEADS])
        gmax_sb = s.sb("gmax", [P, HEADS])
        rows = s.sb("rows", [P, 2, GC], I32)
        idx = s.sb("idx", [P, 2, GC], I32)
        lowi = s.sb("lowi", [P, GC], I32)
        low = s.sb("low", [P, 2, GC])
        got = s.sb("got", [P, 2, GC, ROW])
        oh = s.sb("oh", [P, GC, P])
        oht = s.sb("oht", [P, GC, P])
        dst_blk = s.sb("dst_blk", [P, HEADS])
        dst_e = s.sb("dst_e", [P, GC, HEADS])
        e_a = s.sb("e_a", [P, GC, HEADS])
        e_b = s.sb("e_b", [P, GC, HEADS])
        msg = s.sb("msg", [P, GC, ROW])
        scores = s.sb("scores", [P, tiles, E])
        pick = [s.sb(f"pick{k}", [P, tiles, E]) for k in range(2)]
        b_t = s.bank("b_t")
        b_d = s.bank("b_d")
        b_s = s.bank("b_s")

        weights = s.sem("weights")
        consts = s.sem("consts")
        own = s.sem("own")
        table_ready = s.sem("table_ready")
        table_out = s.sem("table_out")
        top_ready = s.sem("top_ready")
        top_all = s.sem("top_all")
        self_ready = s.sem("self_ready")
        self_exp = s.sem("self_exp")
        rows_in = [s.sem(f"rows_in{k}") for k in range(2)]
        idx_ready = s.sem("idx_ready")
        turn = s.sem("turn")
        gathered = [s.sem(f"gathered{k}") for k in range(2)]
        oh_ready = s.sem("oh_ready")
        oh_turned = s.sem("oh_turned")
        oht_ready = s.sem("oht_ready")
        dst_done = s.sem("dst_done")
        e_ready = s.sem("e_ready")
        ee_ready = s.sem("ee_ready")
        msg_ready = s.sem("msg_ready")
        sum_done = s.sem("sum_done")
        diff_ready = s.sem("diff_ready")
        diff_exp = s.sem("diff_exp")
        block = s.block()

        slots_view = sorted_edges.rearrange("(g p c) o -> g p (c o)", p=P, c=GC)

        def pairs_of(eng):
            return eng.value_load(groups_keep[0:1, gmax:gmax + 1], min_val=1, max_val=gmax // 2)

        @block.sync
        def _(sp):
            for dst, src, n in ((att_src, "att_src", HC), (att_dst, "att_dst", HC), (b_gat, "b_gat", HC),
                                (gamma, "ln_gamma", HC), (beta, "ln_beta", HC)):
                sp.dma_start(dst[:, :], rows_of(w[src], n)).then_inc(weights, 16)
            sp.wait_ge(table_ready, 1)
            sp.dma_start(table.rearrange("(t n) f -> n t f", n=P), hk[:, :, :]).then_inc(table_out, 16)
            for k in range(2):
                sp.dma_start(rows[:, k, :], slots_view[k]).then_inc(rows_in[k], 16)
            n = pairs_of(sp)
            with sp.Fori(0, n) as i:
                for k in range(2):
                    sp.wait_ge(idx_ready, 2 * i + k + 1)
                    sp.dma_start(rows[:, k, :], slots_view[bass.ds(2 * i + 2 + k, 1)].rearrange("g p c -> p (g c)"))\
                        .then_inc(rows_in[k], 16)
            sp.wait_ge(table_out, 16)
            for k in range(2):
                sp.wait_ge(rows_in[k], 16 * n + 16)
                sp.sem_inc(turn, 1)

        @block.gpsimd
        def _(pool):
            pool.memset(ident[:, :], 0.0).then_inc(consts, 1)
            pool.wait_ge(consts, 1)
            pool.affine_select(out=ident[:, :], in_=ident[:, :], compare_op=ALU.not_equal, fill=1.0,
                               base=0, pattern=[[-1, P]], channel_multiplier=1).then_inc(consts, 1)
            pool.iota(iota_f[:, :], [[1, P]], base=0, channel_multiplier=0,
                      allow_small_or_imprecise_dtypes=True).then_inc(consts, 1)
            pool.wait_ge(top_ready, 1)
            pool.partition_all_reduce(gmax_sb[:, :], top[:, :], P, bass.bass_isa.ReduceOp.max).then_inc(top_all, 1)
            pool.wait_ge(table_out, 16)
            n = pairs_of(pool)
            with pool.Fori(0, n) as i:
                for k in range(2):
                    pool.wait_ge(idx_ready, 2 * i + k + 1)
                    pool.sem_inc(turn, 1)
                    for c in range(GC):
                        pool.indirect_dma_start(
                            out=got[:, k, c, :], out_offset=None, in_=table,
                            in_offset=bass.IndirectOffsetOnAxis(ap=idx[:, k, c:c + 1].bitcast(U32), axis=0))\
                            .then_inc(gathered[k], 16)

        @block.tensor
        def _(pe):
            pe.wait_ge(consts, 3)
            n = pairs_of(pe)
            with pe.Fori(0, n) as i:
                for k in range(2):
                    g = 2 * i + k
                    pe.wait_ge(oh_ready, g + 1)
                    for c in range(GC):
                        mm = pe.transpose(b_t[:, P * c:P * c + P], oh[:, c, :], ident[:, :])
                    mm.then_inc(oh_turned, 1)
                    pe.wait_ge(oht_ready, g + 1)
                    for c in range(GC):
                        mm = pe.matmul(b_d[:, HEADS * c:HEADS * c + HEADS], oht[:, c, :], dst_blk[:, :],
                                       start=True, stop=True)
                    mm.then_inc(dst_done, 1)
                    pe.wait_ge(msg_ready, g + 1)
                    for c in range(GC):
                        mm = pe.matmul(b_s[:, 0:ROW], oh[:, c, :], msg[:, c, :], start=(c == 0), stop=(c == GC - 1))
                    mm.then_inc(sum_done, 1)

        @block.scalar
        def _(act):
            act.wait_ge(self_ready, 1)
            act.activation(self_e[:, :, :], self_e[:, :, :], ACT.Exp).then_inc(self_exp, 1)
            n = pairs_of(act)
            with act.Fori(0, n) as i:
                for k in range(2):
                    g = 2 * i + k
                    act.wait_ge(oh_turned, g + 1)
                    act.activation(flat(oht[:, :, :]), b_t[:, :], ACT.Copy).then_inc(oht_ready, 1)
                    act.wait_ge(e_ready, g + 1)
                    act.activation(msg[:, :, HC:ROW], e_a[:, :, :], ACT.Exp).then_inc(ee_ready, 1)
            act.wait_ge(diff_ready, 1)
            act.activation(small2[:, :], small2[:, :], ACT.Exp).then_inc(diff_exp, 1)

        @block.vector
        def _(v):
            me = Done(v, own)
            v.wait_ge(weights, 16 * 5)
            v.wait_ge(consts, 3)
            h = hk[:, :, 0:HC]
            T3 = [P, tiles, HC]
            me.link(v.tensor_tensor(prod[:, :, :], h, over(att_src[:, :].unsqueeze(1), T3), ALU.mult))
            me.link(v.tensor_reduce(hk[:, :, HC:ROW], prod[:, :, :].rearrange("p t (h c) -> p t h c", c=CH),
                                    AX.X, ALU.add))
            me.link(v.tensor_tensor(prod[:, :, :], h, over(att_dst[:, :].unsqueeze(1), T3), ALU.mult))
            v.tensor_reduce(dst_keep[:, :, :], prod[:, :, :].rearrange("p t (h c) -> p t h c", c=CH),
                            AX.X, ALU.add).then_inc(table_ready, 1)
            v.wait_ge(table_ready, 1)
            v.tensor_reduce(top[:, :], hk[:, :, HC:ROW].rearrange("p t h -> p h t"), AX.X, ALU.max)\
                .then_inc(top_ready, 1)
            v.wait_ge(top_all, 1)
            top_b = over(gmax_sb[:, :].unsqueeze(1), [P, tiles, HEADS])
            me.link(v.tensor_tensor(bound[:, :, :], dst_keep[:, :, :], top_b, ALU.add))
            me.link(v.scalar_tensor_tensor(out=bound[:, :, :], in0=bound[:, :, :], scalar=SLOPE,
                                           in1=bound[:, :, :], op0=ALU.mult, op1=ALU.max))
            me.link(v.tensor_tensor(self_e[:, :, :], hk[:, :, HC:ROW], dst_keep[:, :, :], ALU.add))
            me.link(v.scalar_tensor_tensor(out=self_e[:, :, :], in0=self_e[:, :, :], scalar=SLOPE,
                                           in1=self_e[:, :, :], op0=ALU.mult, op1=ALU.max))
            v.tensor_tensor(self_e[:, :, :], self_e[:, :, :], bound[:, :, :], ALU.subtract).then_inc(self_ready, 1)
            v.wait_ge(self_exp, 1)
            me.link(v.tensor_copy(acc[:, :, HC:ROW], self_e[:, :, :]))
            me.link(v.tensor_tensor(acc[:, :, 0:HC].rearrange("p t (h c) -> p t h c", c=CH),
                                    hk[:, :, 0:HC].rearrange("p t (h c) -> p t h c", c=CH),
                                    over(self_e[:, :, :].unsqueeze(3), [P, tiles, HEADS, CH]), ALU.mult))

            def indices(i, k):
                v.wait_ge(rows_in[k], 16 * i + 16)
                me.link(v.tensor_scalar(idx[:, k, :], rows[:, k, :], 7, nodes - 1, ALU.logical_shift_right,
                                        ALU.bitwise_and))
                v.scalar_tensor_tensor(out=low[:, k, :], in0=idx[:, k, :], scalar=-float(P), in1=rows[:, k, :],
                                       op0=ALU.mult, op1=ALU.add).then_inc(idx_ready, 1)

            def onehots(g, k):
                v.wait_ge(idx_ready, g + 1)
                blk = v.value_load(groups_keep[0:1, bass.ds(g, 1)], min_val=0, max_val=tiles - 1)
                me.link(v.tensor_copy(dst_blk[:, :], dst_keep[:, bass.ds(blk, 1), :].rearrange("p a h -> p (a h)")))
                for c in range(GC):
                    ins = v.tensor_scalar(oh[:, c, :], iota_f[:, :], low[:, k, c:c + 1], None, ALU.is_equal)
                ins.then_inc(oh_ready, 1)

            def messages(i, k):
                g = 2 * i + k
                v.wait_ge(dst_done, g + 1)
                me.link(v.tensor_copy(dst_e[:, :, :], b_d[:, 0:GC * HEADS].rearrange("p (c h) -> p c h", h=HEADS)))
                me.link(v.tensor_tensor(e_b[:, :, :], dst_e[:, :, :], over(gmax_sb[:, :].unsqueeze(1), [P, GC, HEADS]),
                                        ALU.add))
                me.link(v.scalar_tensor_tensor(out=e_b[:, :, :], in0=e_b[:, :, :], scalar=SLOPE, in1=e_b[:, :, :],
                                               op0=ALU.mult, op1=ALU.max))
                v.wait_ge(gathered[k], (16 * GC) * i + 16 * GC)
                me.link(v.tensor_tensor(e_a[:, :, :], dst_e[:, :, :], got[:, k, :, HC:ROW], ALU.add))
                me.link(v.scalar_tensor_tensor(out=e_a[:, :, :], in0=e_a[:, :, :], scalar=SLOPE, in1=e_a[:, :, :],
                                               op0=ALU.mult, op1=ALU.max))
                v.tensor_tensor(e_a[:, :, :], e_a[:, :, :], e_b[:, :, :], ALU.subtract).then_inc(e_ready, 1)
                v.wait_ge(ee_ready, g + 1)
                v.tensor_tensor(msg[:, :, 0:HC].rearrange("p c (h f) -> p c h f", f=CH),
                                got[:, k, :, 0:HC].rearrange("p c (h f) -> p c h f", f=CH),
                                over(msg[:, :, HC:ROW].unsqueeze(3), [P, GC, HEADS, CH]), ALU.mult)\
                    .then_inc(msg_ready, 1)
                blk = v.value_load(groups_keep[0:1, bass.ds(g, 1)], min_val=0, max_val=tiles - 1)
                v.wait_ge(sum_done, g + 1)
                here = acc[:, bass.ds(blk, 1), :].rearrange("p a f -> p (a f)")
                me.link(v.tensor_tensor(here, here, b_s[:, 0:ROW], ALU.add))

            indices(0, 0)
            onehots(0, 0)
            first = me.n
            per = 16
            n = pairs_of(v)
            with v.Fori(0, n) as i:
                me.base, me.n = first + per * i, 0
                for k in range(2):
                    indices(i + k, 1 - k)
                    messages(i, k)
                    onehots(2 * i + k + 1, 1 - k)
                assert me.n == per, me.n
            fin = Done(v, s.sem("own2"))
            acc_h = acc[:, :, 0:HC].rearrange("p t (h c) -> p t h c", c=CH)
            fin.link(v.tensor_scalar(acc[:, :, HC:ROW], acc[:, :, HC:ROW], 1e-16, None, ALU.add))
            fin.link(v.reciprocal(self_e[:, :, :], acc[:, :, HC:ROW]))
            fin.link(v.tensor_tensor(prod[:, :, :].rearrange("p t (h c) -> p t h c", c=CH), acc_h,
                                     over(self_e[:, :, :].unsqueeze(3), [P, tiles, HEADS, CH]), ALU.mult))
            fin.link(v.tensor_tensor(prod[:, :, :], prod[:, :, :], over(b_gat[:, :].unsqueeze(1), T3), ALU.add))
            fin.link(v.tensor_reduce(small[:, :], prod[:, :, :], AX.X, ALU.add))
            fin.link(v.tensor_scalar(small[:, :], small[:, :], 1.0 / HC, None, ALU.mult))
            fin.link(v.tensor_tensor(prod[:, :, :], prod[:, :, :], over(small[:, :].unsqueeze(2), T3), ALU.subtract))
            sq = acc[:, :, 0:HC]
            fin.link(v.tensor_tensor(sq, prod[:, :, :], prod[:, :, :], ALU.mult))
            fin.link(v.tensor_reduce(small[:, :], sq, AX.X, ALU.add))
            fin.link(v.tensor_scalar(small[:, :], small[:, :], 1.0 / HC, LN_EPS, ALU.mult, ALU.add))
            rsqrt(fin, v, small[:, :], small2[:, :], rs[:, :])
            fin.link(v.tensor_tensor(prod[:, :, :], prod[:, :, :], over(rs[:, :].unsqueeze(2), T3), ALU.mult))
            fin.link(v.tensor_tensor(prod[:, :, :], prod[:, :, :], over(gamma[:, :].unsqueeze(1), T3), ALU.mult))
            fin.link(v.tensor_tensor(prod[:, :, :], prod[:, :, :], over(beta[:, :].unsqueeze(1), T3), ALU.add))
            fin.link(v.tensor_reduce(scores[:, :, :], prod[:, :, :].rearrange("p t (h c) -> p t c h", c=CH),
                                     AX.X, ALU.add))
            fin.link(v.tensor_scalar(scores[:, :, :], scores[:, :, :], 1.0 / HEADS, None, ALU.mult))
            top_two(v, fin, scores, pick, small, small2, bound)
            v.tensor_tensor(small2[:, :], small2[:, :], small[:, :], ALU.subtract).then_inc(diff_ready, 1)
            v.wait_ge(diff_exp, 1)
            fin.link(v.tensor_scalar(small[:, :], small2[:, :], 1.0, None, ALU.add))
            fin.link(v.reciprocal(small[:, :], small[:, :]))
            fin.link(v.tensor_tensor(small2[:, :], small2[:, :], small[:, :], ALU.mult))
            T4 = [P, tiles, E]
            fin.link(v.tensor_tensor(pick[0][:, :, :], pick[0][:, :, :], over(small[:, :].unsqueeze(2), T4), ALU.mult))
            fin.link(v.tensor_tensor(pick[1][:, :, :], pick[1][:, :, :], over(small2[:, :].unsqueeze(2), T4), ALU.mult))
            fin.link(v.tensor_tensor(gates[:, :, 0:E], pick[0][:, :, :], pick[1][:, :, :], ALU.add))


def top_two(v, me, scores, pick, first, second, work):
    E = scores.shape[2]
    tiles = scores.shape[1]
    BIG = 3.0e38
    found, eq, = work[:, :, 0], work[:, :, 1]
    for r, (mask, best) in enumerate(((pick[0], first), (pick[1], second))):
        src = scores if r == 0 else pick[1]
        me.link(v.tensor_reduce(best[:, :], src[:, :, :], AX.X, ALU.max))
        me.link(v.memset(found, 0.0))
        for e in range(E):
            me.link(v.tensor_tensor(eq, src[:, :, e], best[:, :], ALU.is_equal))
            me.link(v.tensor_tensor(mask[:, :, e], eq, found, ALU.is_gt))
            me.link(v.tensor_tensor(found, found, eq, ALU.max))
        if r == 0:
            me.link(v.scalar_tensor_tensor(out=pick[1][:, :, :], in0=pick[0][:, :, :], scalar=-BIG,
                                           in1=scores[:, :, :], op0=ALU.mult, op1=ALU.add))


def dense_attention(nc, adj, w, keep):
    x_keep, xt_keep, logits_keep = keep["x"], keep["xt"], keep["logits"]
    tiles = x_keep.shape[1]
    groups = tiles // TB
    E = w["gate_w"].shape[1]
    with Scope(nc, "gat") as s:
        ident = s.sb("ident", [P, P])
        adj_sb = s.sb("adj", [P, 2, TB, P])
        xn = s.sb("xn", [P, TB, P])
        xt = s.sb("xt", [P, TB, P])
        h = s.sb("h", [P, TB, P])
        ha = s.sb("ha", [P, TB, P])
        lg = s.sb("lg", [P, TB, P])
        off = s.sb("off", [P, TB, P])
        att = s.sb("att", [P, TB, P])
        att_t = s.sb("att_t", [P, TB, P])
        hp = s.sb("hp", [P, TB, P])
        hm = s.sb("hm", [P, TB, P])
        stats = s.sb("stats", [P, TB, 6])
        mv = s.sb("mv", [P, TB, 4])
        rstd = s.sb("rstd", [P, TB])
        sc = s.sb("sc", [P, TB])
        sc2 = s.sb("sc2", [P, TB])
        negmax = s.sb("negmax", [P, TB])
        den = s.sb("den", [P, TB])
        rden = s.sb("rden", [P, TB])
        wh = s.sb("wh", [P, P])
        a1 = s.sb("a1", [P, P])
        a2 = s.sb("a2", [P, P])
        gw = s.sb("gw", [P, E])
        gb = s.sb("gb", [P, E])
        b_x = s.bank("b_x")
        b_h = s.bank("b_h")
        b_a = s.bank("b_a")
        b_o = s.bank("b_o")
        b_xt = s.bank("b_xt")
        b_p = s.bank("b_p")
        weights = s.sem("weights")
        consts = s.sem("consts")
        own = s.sem("own")
        turn = s.sem("turn")
        arrived = [s.sem(f"arrived{k}") for k in range(2)]
        adj_used = s.sem("adj_used")
        xn_ready = s.sem("xn_ready")
        xn_turned = s.sem("xn_turned")
        xt_ready = s.sem("xt_ready")
        h_done = s.sem("h_done")
        h_ready = s.sem("h_ready")
        max_ready = s.sem("max_ready")
        att_ready = s.sem("att_ready")
        att_turned = s.sem("att_turned")
        att_t_ready = s.sem("att_t_ready")
        out_done = s.sem("out_done")
        hm_ready = s.sem("hm_ready")
        exp_ready = s.sem("exp_ready")
        norm_ready = s.sem("norm_ready")
        x_turned = s.sem("x_turned")
        xt2_ready = s.sem("xt2_ready")
        xt_kept = s.sem("xt_kept")
        proj_done = s.sem("proj_done")
        proj_kept = s.sem("proj_kept")
        block = s.block()
        av = adj.rearrange("t n m -> n t m")

        @block.sync
        def _(sp):
            for dst, src in ((wh[:, :], w["W"]), (a1[:, :], rows_of(w["a"][0:P, 0], P)),
                             (a2[:, :], rows_of(w["a"][P:2 * P, 0], P)), (gw[:, :], w["gate_w"]),
                             (gb[:, :], rows_of(w["gate_b"], E))):
                sp.dma_start(dst, src).then_inc(weights, 16)
            for k in range(2):
                sp.dma_start(adj_sb[:, k, :, :], av[:, k * TB:k * TB + TB, :]).then_inc(arrived[k], 16)
            with sp.Fori(0, groups // 2 - 1) as i:
                for k in range(2):
                    sp.wait_ge(adj_used, 2 * i + k + 1)
                    sp.dma_start(adj_sb[:, k, :, :], av[:, bass.ds(2 * TB * i + 2 * TB + k * TB, TB), :])\
                        .then_inc(arrived[k], 16)

        @block.gpsimd
        def _(pool):
            pool.memset(ident[:, :], 0.0).then_inc(consts, 1)
            pool.wait_ge(consts, 1)
            pool.affine_select(out=ident[:, :], in_=ident[:, :], compare_op=ALU.not_equal, fill=1.0,
                               base=0, pattern=[[-1, P]], channel_multiplier=1).then_inc(consts, 1)
            with pool.Fori(0, groups) as g:
                pool.wait_ge(xt2_ready, g + 1)
                pool.tensor_copy(xt_keep[:, bass.ds(g * TB, TB), :], xt[:, :, :]).then_inc(xt_kept, 1)

        @block.tensor
        def _(pe):
            pe.wait_ge(weights, 16 * 5)
            pe.wait_ge(consts, 2)
            with pe.Fori(0, groups) as g:
                pe.wait_ge(xn_ready, g + 1)
                for j in range(TB):
                    mm = pe.transpose(b_x[:, P * j:P * j + P], xn[:, j, :], ident[:, :])
                mm.then_inc(xn_turned, 1)
                pe.wait_ge(xt_ready, g + 1)
                for j in range(TB):
                    mm = pe.matmul(b_h[:, P * j:P * j + P], xt[:, j, :], wh[:, :], start=True, stop=True)
                mm.then_inc(h_done, 1)
                pe.wait_ge(att_ready, g + 1)
                for j in range(TB):
                    mm = pe.transpose(b_a[:, P * j:P * j + P], att[:, j, :], ident[:, :])
                mm.then_inc(att_turned, 1)
                pe.wait_ge(att_t_ready, g + 1)
                for j in range(TB):
                    mm = pe.matmul(b_o[:, P * j:P * j + P], att_t[:, j, :], h[:, j, :], start=True, stop=True)
                mm.then_inc(out_done, 1)
                pe.wait_ge(norm_ready, g + 1)
                for j in range(TB):
                    mm = pe.transpose(b_xt[:, P * j:P * j + P], xn[:, j, :], ident[:, :])
                mm.then_inc(x_turned, 1)
                pe.wait_ge(xt2_ready, g + 1)
                for j in range(TB):
                    mm = pe.matmul(b_p[:, E * j:E * j + E], xt[:, j, :], gw[:, :], start=True, stop=True)
                mm.then_inc(proj_done, 1)

        @block.scalar
        def _(act):
            with act.Fori(0, groups) as g:
                act.wait_ge(xn_turned, g + 1)
                act.wait_ge(xt_kept, g + 1)
                act.activation(flat(xt[:, :, :]), b_x[:, :], ACT.Copy).then_inc(xt_ready, 1)
                act.wait_ge(h_done, g + 1)
                act.activation(flat(h[:, :, :]), b_h[:, :], ACT.Copy).then_inc(h_ready, 1)
                act.wait_ge(max_ready, g + 1)
                for j in range(TB):
                    ins = act.activation(att[:, j, :], lg[:, j, :], ACT.Exp, bias=negmax[:, j:j + 1],
                                         accum_out=den[:, j:j + 1])
                ins.then_inc(att_ready, 1)
                act.wait_ge(att_turned, g + 1)
                act.activation(flat(att_t[:, :, :]), b_a[:, :], ACT.Copy).then_inc(att_t_ready, 1)
                act.wait_ge(hm_ready, g + 1)
                act.activation(flat(hm[:, :, :]), flat(hm[:, :, :]), ACT.Exp).then_inc(exp_ready, 1)
                act.wait_ge(x_turned, g + 1)
                act.activation(flat(xt[:, :, :]), b_xt[:, :], ACT.Copy).then_inc(xt2_ready, 1)

        @block.vector
        def _(v):
            me = Done(v, own)
            v.wait_ge(weights, 16 * 5)
            v.wait_ge(consts, 2)
            v.sem_inc(xt_kept, 1)
            me.link(v.tensor_tensor(a1[:, :], a1[:, :], a2[:, :], ALU.add))
            per = 33+22
            T = [P, TB, P]
            with v.Fori(0, groups // 2) as i:
                for k in range(2):
                    g = 2 * i + k
                    me.base, me.n = 1 + per * g, 0
                    src = x_keep[:, bass.ds(g * TB, TB), :]
                    srcs = [src[:, j, :] for j in range(TB)]
                    norm_rows(v, me, turn, srcs, stats, mv, rstd, xn).then_inc(xn_ready, 1)
                    v.wait_ge(h_ready, g + 1)
                    me.link(v.tensor_tensor(ha[:, :, :], h[:, :, :], over(a1[:, :].unsqueeze(1), T), ALU.mult))
                    me.link(v.tensor_reduce(sc[:, :], ha[:, :, :], AX.X, ALU.add))
                    me.link(v.scalar_tensor_tensor(out=sc2[:, :], in0=sc[:, :], scalar=SLOPE, in1=sc[:, :],
                                                   op0=ALU.mult, op1=ALU.max))
                    v.wait_ge(arrived[k], 16 * i + 16)
                    for j in range(TB):
                        me.mark(v.tensor_scalar(lg[:, j, :], adj_sb[:, k, j, :], 0.0, sc2[:, j:j + 1],
                                                ALU.is_gt, ALU.mult))
                    me.mark(v.tensor_scalar(off[:, :, :], adj_sb[:, k, :, :], 0.0, NEG, ALU.is_le, ALU.mult))
                    me.wait()
                    v.tensor_tensor(lg[:, :, :], lg[:, :, :], off[:, :, :], ALU.add).then_inc(adj_used, 1)
                    v.wait_ge(adj_used, g + 1)
                    v.tensor_reduce(negmax[:, :], lg[:, :, :], AX.X, ALU.max, negate=True).then_inc(max_ready, 1)
                    v.wait_ge(att_ready, g + 1)
                    me.link(v.reciprocal(rden[:, :], den[:, :]))
                    v.wait_ge(out_done, g + 1)
                    for j in range(TB):
                        me.mark(v.tensor_scalar(hp[:, j, :], b_o[:, P * j:P * j + P], rden[:, j:j + 1], None,
                                                ALU.mult))
                    me.wait()
                    v.tensor_scalar(hm[:, :, :], hp[:, :, :], 0.0, None, ALU.min).then_inc(hm_ready, 1)
                    me.link(v.scalar_tensor_tensor(out=src, in0=hp[:, :, :], scalar=0.0, in1=src,
                                                   op0=ALU.max, op1=ALU.add))
                    v.wait_ge(exp_ready, g + 1)
                    me.link(v.scalar_tensor_tensor(out=src, in0=hm[:, :, :], scalar=-1.0, in1=src,
                                                   op0=ALU.add, op1=ALU.add))
                    norm_rows(v, me, turn, srcs, stats, mv, rstd, xn).then_inc(norm_ready, 1)
                    v.wait_ge(proj_done, g + 1)
                    v.tensor_tensor(logits_keep[:, bass.ds(g * TB, TB), :],
                                    b_p[:, 0:TB * E].rearrange("p (a b) -> p a b", a=TB),
                                    over(gb[:, :].unsqueeze(1), [P, TB, E]), ALU.add).then_inc(proj_kept, 1)
                    n = me.n
            assert n == per, n


def experts(nc, tag, w, keep, softmax_gates, out):
    W1, b1, W2, b2 = w["W1"], w["b1"], w["W2"], w["b2"]
    E, D, H = W1.shape
    HK = H // P
    x_keep, xt_keep, gates = keep["x"], keep["xt"], keep["gates"]
    tiles = x_keep.shape[1]
    groups = tiles // TB
    N = TB * P
    with Scope(nc, tag) as s:
        ident = s.sb("ident", [P, P])
        w1 = s.sb("w1", [P, E, H])
        w2 = s.sb("w2", [P, E * HK, D])
        b1c = s.sb("b1c", [P, E * HK])
        b2r = s.sb("b2r", [E, D])
        gate = s.sb("gate", [P, TB, E])
        gate_t = s.sb("gate_t", [E, N])
        hid = [s.sb(f"hid{k}", [P, HK, N]) for k in range(2)]
        acc = s.sb("acc", [P, TB, D])
        b_z = [s.bank(f"b_z{k}") for k in range(4)]
        b_y = [s.bank(f"b_y{k}") for k in range(2)]
        b_g = s.bank("b_g")
        b_b = s.bank("b_b")
        weights = s.sem("weights")
        consts = s.sem("consts")
        own = s.sem("own")
        gates_ready = s.sem("gates_ready")
        gate_ready = s.sem("gate_ready")
        gate_turned = s.sem("gate_turned")
        gate_t_ready = s.sem("gate_t_ready")
        bias_done = s.sem("bias_done")
        z_done = s.sem("z_done")
        hid_ready = s.sem("hid_ready")
        y_done = s.sem("y_done")
        y_added = s.sem("y_added")
        stored = s.sem("stored")
        shifted = s.sem("shifted")
        turn = s.sem("turn")
        exped = s.sem("exped")
        block = s.block()

        @block.sync
        def _(sp):
            sp.dma_start(w1[:, :, :], W1.rearrange("e d h -> d e h")).then_inc(weights, 16)
            sp.dma_start(w2[:, :, :], W2.rearrange("e (k p) d -> p (e k) d", p=P)).then_inc(weights, 16)
            sp.dma_start(b1c[:, :], b1.rearrange("e (k p) -> p (e k)", p=P),
                         allow_slow_non_contiguous=True).then_inc(weights, 16)
            sp.dma_start(b2r[:, :], b2).then_inc(weights, 16)
            if out is not None:
                ov = out.rearrange("t n d -> n t d")
                with sp.Fori(0, groups) as g:
                    sp.wait_ge(y_added, g * E + E)
                    sp.dma_start(ov[:, bass.ds(g * TB, TB), :], x_keep[:, bass.ds(g * TB, TB), :])\
                        .then_inc(stored, 16)
                sp.wait_ge(stored, 16 * groups)

        @block.gpsimd
        def _(pool):
            pool.memset(ident[:, :], 0.0).then_inc(consts, 1)
            pool.wait_ge(consts, 1)
            pool.affine_select(out=ident[:, :], in_=ident[:, :], compare_op=ALU.not_equal, fill=1.0,
                               base=0, pattern=[[-1, P]], channel_multiplier=1).then_inc(consts, 1)

        @block.tensor
        def _(pe):
            pe.wait_ge(weights, 64)
            pe.wait_ge(consts, 2)
            with pe.Fori(0, groups) as g:
                def up(e):
                    for c in range(HK):
                        n = e * HK + c
                        if n >= 4:
                            pe.wait_ge(hid_ready, g * (E * HK) + n - 3)
                        pe.matmul(b_z[n % 4][:, :], w1[:, e, P * c:P * c + P],
                                  flat(xt_keep[:, bass.ds(g * TB, TB), :]), start=True, stop=True)\
                            .then_inc(z_done, 1)

                def down(e):
                    pe.wait_ge(hid_ready, g * (E * HK) + (e + 1) * HK)
                    if e >= 2:
                        pe.wait_ge(y_added, g * E + e - 1)
                    for j in range(TB):
                        for c in range(HK):
                            mm = pe.matmul(b_y[e % 2][:, P * j:P * j + P], hid[e % 2][:, c, P * j:P * j + P],
                                           w2[:, e * HK + c, :], start=(c == 0), stop=(c == HK - 1))
                    mm.then_inc(y_done, 1)

                up(0)
                pe.wait_ge(gate_ready, g + 1)
                for j in range(TB):
                    mm = pe.transpose(b_g[0:E, P * j:P * j + P], gate[:, j, :], ident[:, :])
                mm.then_inc(gate_turned, 1)
                up(1)
                pe.wait_ge(gate_t_ready, g + 1)
                for j in range(TB):
                    mm = pe.matmul(b_b[:, P * j:P * j + P], gate_t[:, P * j:P * j + P], b2r[:, :],
                                   start=True, stop=True)
                mm.then_inc(bias_done, 1)
                for e in range(E):
                    if e + 2 < E:
                        down(e)
                        up(e + 2)
                    else:
                        down(e)

        @block.scalar
        def _(act):
            act.wait_ge(weights, 64)
            if softmax_gates:
                act.wait_ge(shifted, 1)
                act.activation(gates[:, :, 0:E], gates[:, :, 0:E], ACT.Exp).then_inc(exped, 1)
            with act.Fori(0, groups) as g:
                for e in range(E):
                    for c in range(HK):
                        n = e * HK + c
                        act.wait_ge(z_done, g * (E * HK) + n + 1)
                        if e >= 2:
                            act.wait_ge(y_done, g * E + e - 1)
                        act.activation(hid[e % 2][:, c, :], b_z[n % 4][:, :], ACT.Gelu,
                                       bias=b1c[:, n:n + 1]).then_inc(hid_ready, 1)

        @block.vector
        def _(v):
            me = Done(v, own)
            if softmax_gates:
                with Scope(nc, tag + "_gates") as t:
                    best = t.sb("best", [P, tiles])
                    best2 = t.sb("best2", [P, tiles])
                    pick = [t.sb(f"pick{k}", [P, tiles, E]) for k in range(2)]
                    work = t.sb("work", [P, tiles, 2])
                T3 = [P, tiles, E]
                gl = gates[:, :, 0:E]
                me.link(v.tensor_reduce(best[:, :], gl, AX.X, ALU.max))
                v.tensor_tensor(gl, gl, over(best[:, :].unsqueeze(2), T3), ALU.subtract).then_inc(shifted, 1)
                v.wait_ge(exped, 1)
                me.link(v.tensor_reduce(best[:, :], gl, AX.X, ALU.add))
                me.link(v.reciprocal(best[:, :], best[:, :]))
                me.link(v.tensor_tensor(gl, gl, over(best[:, :].unsqueeze(2), T3), ALU.mult))
                top_two(v, me, gates, pick, best, best2, work)
                me.link(v.tensor_tensor(pick[0][:, :, :], pick[0][:, :, :], pick[1][:, :, :], ALU.add))
                me.link(v.tensor_tensor(gl, gl, pick[0][:, :, :], ALU.mult))
            first = me.n
            per = 1 + (TB - 1) * (E - 1)
            with v.Fori(0, groups) as g:
                me.base, me.n = first + per * g, 0
                xs = x_keep[:, bass.ds(g * TB, TB), :]
                v.tensor_copy(gate[:, :, :], gates[:, bass.ds(g * TB, TB), 0:E]).then_inc(gate_ready, 1)
                v.wait_ge(gate_turned, g + 1)
                v.tensor_copy(gate_t[:, :], b_g[0:E, :]).then_inc(gate_t_ready, 1)
                v.wait_ge(bias_done, g + 1)
                me.link(v.tensor_tensor(acc[:, :, :], xs, b_b[:, :].rearrange("p (a b) -> p a b", a=TB), ALU.add))
                for e in range(E):
                    v.wait_ge(y_done, g * E + e + 1)
                    for j in range(TB):
                        ins = v.scalar_tensor_tensor(out=acc[:, j, :] if e < E - 1 else xs[:, j, :],
                                                     in0=b_y[e % 2][:, P * j:P * j + P], scalar=gate[:, j, e:e + 1],
                                                     in1=acc[:, j, :], op0=ALU.mult, op1=ALU.add)
                        if e < E - 1 and j < TB - 1:
                            me.mark(ins)
                    if e < E - 1:
                        ins.then_inc(y_added, 1)
                        me.wait()
                        v.wait_ge(y_added, g * E + e + 1)
                    else:
                        ins.then_inc(y_added, 1)
                        v.wait_ge(y_added, g * E + e + 1)
                        v.sem_inc(turn, 1)


def network(nc, t, out):
    x, adj = t["x"], t["adj"]
    tiles = x.shape[0]
    nodes = tiles * P
    n_edges = t["L0_ffn_edge_index"].shape[1]
    gmax = n_edges // GROUP + tiles
    spare = 8
    sorted_edges = nc.dram_tensor("sorted_edges", ((gmax + spare) * GROUP, 1), I32).ap()
    table = nc.dram_tensor("node_table", (nodes, ROW), F32).ap()
    with Scope(nc, "keep") as s:
        keep = {"groups": s.sb("groups", [P, gmax + 1], I32)}
        sort_edges(nc, t["L0_ffn_edge_index"], sorted_edges, keep["groups"], nodes)
        keep["x"] = s.sb("x", [P, tiles, P])
        keep["xt"] = s.sb("xt", [P, tiles, P])
        keep["gates"] = s.sb("gates", [P, tiles, CH])
        with Scope(nc, "edge") as m:
            keep["h"] = m.sb("h", [P, tiles, ROW])
            keep["dst"] = m.sb("dst", [P, tiles, HEADS])
            keep["acc"] = m.sb("acc", [P, tiles, ROW])
            gin_layer(nc, x, adj, {
                "W1": t["L0_gnn_W1"], "b1": t["L0_gnn_b1"], "rms": t["L0_gnn_rms_weight"],
                "W2": t["L0_gnn_W2"], "b2": t["L0_gnn_b2"], "eps": t["L0_gnn_epsilon"],
                "W_gat": t["L0_ffn_W_gat"]}, keep)
            edge_attention(nc, {
                "att_src": t["L0_ffn_att_src"].rearrange("h c -> (h c)"),
                "att_dst": t["L0_ffn_att_dst"].rearrange("h c -> (h c)"),
                "b_gat": t["L0_ffn_b_gat"], "ln_gamma": t["L0_ffn_ln_gamma"],
                "ln_beta": t["L0_ffn_ln_beta"]}, sorted_edges, table, keep)
        experts(nc, "moe0", {"W1": t["L0_ffn_W1"], "b1": t["L0_ffn_b1"], "W2": t["L0_ffn_W2"],
                             "b2": t["L0_ffn_b2"]}, keep, False, None)
        keep["logits"] = s.sb("logits", [P, tiles, t["L1_ffn_gate_w"].shape[1]])
        dense_attention(nc, adj, {"W": t["L1_gnn_W"], "a": t["L1_gnn_a"], "gate_w": t["L1_ffn_gate_w"],
                                  "gate_b": t["L1_ffn_gate_b"]}, keep)
        experts(nc, "moe1", {"W1": t["L1_ffn_W1"], "b1": t["L1_ffn_b1"], "W2": t["L1_ffn_W2"],
                             "b2": t["L1_ffn_b2"]}, dict(keep, gates=keep["logits"]), True, out)


_INS = ["x", "adj", "L0_gnn_epsilon", "L0_gnn_W1", "L0_gnn_b1", "L0_gnn_rms_weight", "L0_gnn_W2", "L0_gnn_b2",
        "L0_ffn_W_gat", "L0_ffn_att_src", "L0_ffn_att_dst", "L0_ffn_b_gat", "L0_ffn_ln_gamma", "L0_ffn_ln_beta",
        "L0_ffn_W1", "L0_ffn_b1", "L0_ffn_W2", "L0_ffn_b2", "L0_ffn_edge_index", "L1_gnn_W", "L1_gnn_a",
        "L1_ffn_gate_w", "L1_ffn_gate_b", "L1_ffn_W1", "L1_ffn_b1", "L1_ffn_W2", "L1_ffn_b2"]


def kernel(**inputs):
    import numpy as _np
    import concourse.bacc as _bacc
    from concourse import mybir as _mybir
    from concourse.bass_utils import run_bass_kernel_spmd as _run

    nc = _bacc.Bacc("TRN2", target_bir_lowering=False, num_devices=1)
    arrays, args = {}, {}
    for name in _INS:
        a = _np.ascontiguousarray(inputs[name])
        if a.ndim == 0:
            a = a.reshape(1)
        arrays[f"in_{name}"] = a
        args[name] = nc.dram_tensor(f"in_{name}", a.shape, _mybir.dt.from_np(a.dtype), kind="ExternalInput").ap()
    shape = _np.shape(inputs["x"])
    out = nc.dram_tensor("out_0", shape, _mybir.dt.float32, kind="ExternalOutput").ap()
    network(nc, args, out)
    r = _run(nc, [arrays], core_ids=[0])
    return r.results[0]["out_0"]
```

```python
from contextlib import ExitStack

import concourse.bass as bass
from concourse import mybir

F32 = mybir.dt.float32
U32 = mybir.dt.uint32
I32 = mybir.dt.int32
BF16 = mybir.dt.bfloat16
ALU = mybir.AluOpType
ACT = mybir.ActivationFunctionType
AX = mybir.AxisListType

P = 128
LN_EPS = 1e-05
RMS_EPS = 1e-06
NEG = -9000000000000000.0
SLOPE = 0.2
TB = 4

HEADS = 4
CH = 4
HC = HEADS * CH
ROW = HC + HEADS

STREAMS = 8
HALF = 2
CHUNKS = HALF * STREAMS
BK = 4
GROUP = 512
GC = GROUP // P
QUAD = 4
EARLY = 94
SPARE = 8


class Scope:

    def __init__(self, nc, tag):
        self.nc, self.tag, self.ctx = nc, tag, ExitStack()

    def __enter__(self):
        return self

    def __exit__(self, *a):
        return self.ctx.__exit__(*a)

    def sb(self, name, shape, dt=F32):
        return self.ctx.enter_context(self.nc.sbuf_tensor(f"{self.tag}_{name}", shape, dt))

    def bank(self, name):
        return self.ctx.enter_context(self.nc.psum_tensor(f"{self.tag}_{name}", [P, 512], F32))

    def sem(self, name):
        return self.ctx.enter_context(self.nc.semaphore(f"{self.tag}_{name}"))

    def block(self):
        return self.ctx.enter_context(self.nc.Block())


class Done:

    def __init__(self, eng, sem):
        self.eng, self.sem, self.base, self.n = eng, sem, 0, 0

    def link(self, ins):
        self.n += 1
        ins.then_inc(self.sem, 1)
        self.eng.wait_ge(self.sem, self.base + self.n)

    def mark(self, ins):
        self.n += 1
        ins.then_inc(self.sem, 1)

    def wait(self):
        self.eng.wait_ge(self.sem, self.base + self.n)


def rows_of(vector_ap, n):
    return vector_ap.rearrange("(a n) -> a n", a=1).broadcast_to([P, n])


def flat(ap):
    return ap.rearrange("p a b -> p (a b)")


def over(ap, shape):
    return ap.broadcast_to(shape)


def scatter_turns(pool, turns, slots, values, slot_now, value_now, staged, turn, scattered, sorted_edges, ready):
    last_slot = pool.to_reg(sorted_edges.shape[0] - 1)

    def half(i, h, first_use):
        at = bass.ds((2 * i + h) * CHUNKS, CHUNKS)
        if ready is not None:
            pool.wait_ge(ready, 4 * i + 2 * h + 2)
            pool.sem_inc(turn, 1)
        if not first_use:
            pool.wait_ge(scattered[h], i * (CHUNKS * 16))
        pool.tensor_copy(slot_now[:, h, :], slots[:, at]).then_inc(staged, 1)
        pool.tensor_copy(value_now[:, h, :], values[:, at]).then_inc(staged, 1)
        pool.wait_ge(staged, 4 * i + 2 * h + 2)
        pool.sem_inc(turn, 1)
        for k in range(CHUNKS):
            pool.indirect_dma_start(
                out=sorted_edges,
                out_offset=bass.IndirectOffsetOnAxis(ap=slot_now[:, h, k:k + 1].bitcast(U32), axis=0),
                in_=value_now[:, h, k:k + 1], in_offset=None,
                bounds_check=last_slot, oob_is_err=False).then_inc(scattered[h], 16)

    for h in range(2):
        half(0, h, True)
    with pool.Fori(1, turns) as i:
        for h in range(2):
            half(i, h, False)
    for h in range(2):
        pool.wait_ge(scattered[h], turns * CHUNKS * 16)


def sort_edges(nc, edge_index, sorted_edges, groups_keep, hub_keep, late, nodes):
    n_edges = edge_index.shape[1]
    cols = n_edges // P
    scols = cols // STREAMS
    iters = scols // (2 * HALF)
    blocks = nodes // P
    gmax = n_edges // GROUP + blocks + SPARE
    slots = sorted_edges.shape[0]
    mark_value = nodes * P
    shift = GROUP.bit_length() - 1

    with Scope(nc, "sort") as s:
        target = s.sb("target", [P, cols], I32)
        packed = s.sb("packed", [P, cols], I32)
        block_of = s.sb("block_of", [P, cols])
        key_of = s.sb("key_of", [P, cols])
        hub_low = s.sb("hub_low", [P, cols])
        hub_key = s.sb("hub_key", [P, 2, 2, CHUNKS])
        hub_oh = s.sb("hub_oh", [P, 2, 2, CHUNKS, P], BF16)
        empty = s.sb("empty", [P, slots // P // 8], I32)
        iota_f = s.sb("iota_f", [P, P])
        iota_b = s.sb("iota_b", [P, P], BF16)
        before = s.sb("before", [P, P], BF16)
        notbefore = s.sb("notbefore", [P, P], BF16)
        ones_b = s.sb("ones_b", [P, P], BF16)
        ones_f = s.sb("ones_f", [P, P])
        zeros_b = s.sb("zeros_b", [P, 512], BF16)
        zeros = s.sb("zeros", [P, P])
        onehot = s.sb("onehot", [P, 2, HALF, STREAMS, P], BF16)
        keycol = s.sb("keycol", [P, 2, CHUNKS])
        slot_f = s.sb("slot_f", [P, 2, CHUNKS])
        dropped = s.sb("dropped", [P, 2, CHUNKS])
        early = [s.sb(name, [P, EARLY * 2 * CHUNKS], I32) for name in ("early_slots", "early_values")]
        slot_now = s.sb("slot_now", [P, 2, CHUNKS], I32)
        value_now = s.sb("value_now", [P, 2, CHUNKS], I32)
        scrap = s.sb("scrap", [P, CHUNKS, P], BF16)
        count = s.sb("count", [P, STREAMS, P])
        total = s.sb("total", [P, P])
        whole = s.sb("whole", [P, P], I32)
        block_end = s.sb("block_end", [P, P])
        start = s.sb("start", [P, STREAMS, P])
        group_iota = s.sb("group_iota", [P, gmax])
        past_end = s.sb("past_end", [P, gmax])
        end_col = s.sb("end_col", [P, 1])
        ranks = [s.bank(f"ranks{k}") for k in range(2)]
        sums = [s.bank(f"sums{k}") for k in range(3)]
        col = s.bank("col")
        hubs = s.bank("hubs")

        loaded = s.sem("loaded")
        filled = s.sem("filled")
        consts = s.sem("consts")
        own = s.sem("own")
        onehot_ready = s.sem("onehot_ready")
        onehot_counted = s.sem("onehot_counted")
        start_ready = s.sem("start_ready")
        end_turned = s.sem("end_turned")
        past_ready = s.sem("past_ready")
        groups_summed = s.sem("groups_summed")
        hub_ready = s.sem("hub_ready")
        hub_counted = s.sem("hub_counted")
        ranked = s.sem("ranked")
        extracted = s.sem("extracted")
        slots_ready = s.sem("slots_ready")
        staged = s.sem("staged")
        turn = s.sem("turn")
        scattered = [s.sem(f"scattered{h}") for h in range(2)]
        block = s.block()

        edges = edge_index.rearrange("t (p c) -> t p c", p=P)

        def bank_of(h, step, k):
            return onehot[:, h, step, BK * k:BK * k + BK, :].rearrange("p a b -> p (a b)")

        @block.sync
        def _(sp):
            sp.dma_start(packed[:, :], edges[0]).then_inc(loaded, 16)
            sp.dma_start(target[:, :], edges[1]).then_inc(loaded, 16)
            sp.wait_ge(consts, 1)
            view = sorted_edges.rearrange("(k p c) o -> k p (c o)", k=8, p=P)
            for k in range(8):
                sp.dma_start(view[k], empty[:, :]).then_inc(filled, 16)
            sp.wait_ge(filled, 8 * 16)

        @block.gpsimd
        def _(pool):
            pool.memset(empty[:, :], mark_value).then_inc(consts, 1)
            pool.iota(iota_f[:, :], [[1, P]], base=0, channel_multiplier=0,
                      allow_small_or_imprecise_dtypes=True).then_inc(consts, 1)
            pool.iota(group_iota[:, :], [[1, gmax]], base=0, channel_multiplier=0,
                      allow_small_or_imprecise_dtypes=True).then_inc(consts, 1)
            pool.memset(ones_b[:, :], 1.0).then_inc(consts, 1)
            pool.memset(ones_f[:, :], 1.0).then_inc(consts, 1)
            pool.memset(zeros[:, :], 0.0).then_inc(consts, 1)
            pool.memset(zeros_b[:, :], 0.0).then_inc(consts, 1)
            pool.wait_ge(consts, 7)
            pool.affine_select(out=before[:, :], in_=ones_b[:, :], compare_op=ALU.is_gt, fill=0.0, base=0,
                               pattern=[[1, P]], channel_multiplier=-1).then_inc(consts, 1)
            pool.affine_select(out=notbefore[:, :], in_=ones_b[:, :], compare_op=ALU.is_ge, fill=0.0, base=0,
                               pattern=[[-1, P]], channel_multiplier=1).then_inc(consts, 1)
            pool.wait_ge(filled, 8 * 16)
            scatter_turns(pool, EARLY, early[0], early[1], slot_now, value_now, staged, turn, scattered,
                          sorted_edges, slots_ready)

        @block.tensor
        def _(pe):
            pe.wait_ge(consts, 9)
            for k in range(2):
                pe.matmul(ranks[k][:, :], ones_b[:, :], zeros_b[:, :], start=True, stop=False,
                          skip_group_check=True)
            with pe.Fori(0, iters) as i:
                for h in range(2):
                    pe.wait_ge(onehot_ready, 2 * i + h + 1)
                    for step in range(HALF):
                        for k in range(2):
                            mm = pe.matmul(ranks[k][:, :], ones_b[:, :], bank_of(h, step, k),
                                           start=False, stop=False, skip_group_check=True)
                    mm.then_inc(onehot_counted, 1)
            pe.wait_ge(start_ready, 1)
            pe.matmul(col[:, 0:1], block_end[0:1, :], ones_f[0:1, 0:1], start=True, stop=True)\
                .then_inc(end_turned, 1)
            for k in range(2):
                pe.matmul(ranks[k][:, :], ones_f[0:1, :],
                          start[0:1, BK * k:BK * k + BK, :].rearrange("p a b -> p (a b)"),
                          start=True, stop=False, skip_group_check=True)
            pe.wait_ge(past_ready, 1)
            for k in range(3):
                w = min(512, gmax - 512 * k)
                mm = pe.matmul(sums[k][:, 0:w], ones_f[:, :], past_end[:, 512 * k:512 * k + w],
                               start=True, stop=True)
            mm.then_inc(groups_summed, 1)
            pe.matmul(hubs[:, :], ones_b[:, :], zeros_b[:, :], start=True, stop=False, skip_group_check=True)
            with pe.Fori(0, iters) as i:
                for h in range(2):
                    pe.wait_ge(onehot_ready, 2 * iters + 2 * i + h + 1)
                    for step in range(HALF):
                        for k in range(2):
                            n = (h * HALF + step) * 2 + k
                            if n > 1:
                                pe.wait_ge(extracted, i * 8 + n - 1)
                                pe.matmul(ranks[k][:, :], notbefore[:, :],
                                          bank_of(h if step else 1 - h, (step - 1) % HALF, k),
                                          start=False, stop=False, skip_group_check=True)
                            pe.matmul(ranks[k][:, :], before[:, :], bank_of(h, step, k),
                                      start=False, stop=False, skip_group_check=True).then_inc(ranked, 1)
                    pe.wait_ge(hub_ready, 2 * i + h + 1)
                    for t in range(CHUNKS):
                        pe.matmul(hubs[:, 0:P], hub_oh[:, h, 0, t, :], hub_oh[:, h, 1, t, :],
                                  start=False, stop=False, skip_group_check=True)
                for k in range(2):
                    pe.wait_ge(extracted, i * 8 + 7 + k)
                    mm = pe.matmul(ranks[k][:, :], notbefore[:, :], bank_of(1, HALF - 1, k),
                                   start=False, stop=False, skip_group_check=True)
                mm.then_inc(hub_counted, 1)

        @block.vector
        def _(v):
            me = Done(v, own)
            v.wait_ge(loaded, 32)
            v.wait_ge(consts, 9)
            v.tensor_copy(iota_b[:, :], iota_f[:, :])
            v.tensor_single_scalar(packed[:, :], packed[:, :], nodes - 1, ALU.min)
            low = block_of[:, :].bitcast(I32)
            me.link(v.tensor_single_scalar(low, target[:, :], P - 1, ALU.bitwise_and))
            me.link(v.tensor_scalar(key_of[:, :], packed[:, :], float(nodes - 1), None, ALU.is_equal))
            me.link(v.scalar_tensor_tensor(out=hub_low[:, :], in0=low, scalar=1.0, in1=key_of[:, :],
                                           op0=ALU.add, op1=ALU.mult))
            me.link(v.tensor_scalar(hub_low[:, :], hub_low[:, :], -1.0, None, ALU.add))
            me.link(v.scalar_tensor_tensor(out=packed[:, :], in0=packed[:, :], scalar=float(P), in1=low,
                                           op0=ALU.mult, op1=ALU.add))
            me.link(v.tensor_single_scalar(target[:, :], target[:, :], 7, ALU.logical_shift_right))
            me.link(v.tensor_copy(block_of[:, :], target[:, :]))
            me.link(v.scalar_tensor_tensor(out=key_of[:, :], in0=key_of[:, :], scalar=float(2 * P), in1=block_of[:, :],
                                           op0=ALU.mult, op1=ALU.add))
            keys = key_of[:, :].rearrange("p (s c) -> p c s", s=STREAMS)
            hub_keys = [a[:, :].rearrange("p (s c) -> p c s", s=STREAMS) for a in (hub_low, block_of)]
            values = packed[:, :].rearrange("p (s c) -> p c s", s=STREAMS)

            def build(c, h):
                me.link(v.tensor_copy(keycol[:, h, :].rearrange("p (a b) -> p a b", a=HALF),
                                      keys[:, bass.ds(c, HALF), :]))
                for t in range(CHUNKS):
                    ins = v.tensor_scalar(onehot[:, h, t // STREAMS, t % STREAMS, :], iota_b[:, :],
                                          keycol[:, h, t:t + 1], None, ALU.is_equal)
                ins.then_inc(onehot_ready, 1)

            for h in range(2):
                build(h * HALF, h)
            first = me.n
            with v.Fori(1, iters) as i:
                me.base, me.n = first + (i - 1) * 2, 0
                for h in range(2):
                    v.wait_ge(onehot_counted, 2 * i + h - 1)
                    build((2 * i + h) * HALF, h)
            me.base, me.n = 0, first + (iters - 1) * 2
            v.wait_ge(onehot_counted, 2 * iters)
            for k in range(2):
                me.link(v.tensor_copy(count[:, BK * k:BK * k + BK, :].rearrange("p a b -> p (a b)"),
                                      ranks[k][:, :]))
            me.link(v.tensor_reduce(total[:, :], count[:, :, :].rearrange("p s b -> p b s"), AX.X, ALU.add))
            me.link(v.tensor_scalar(total[:, :], total[:, :], float(GROUP - 1), None, ALU.add))
            me.link(v.tensor_copy(whole[:, :], total[:, :]))
            me.link(v.tensor_scalar(whole[:, :], whole[:, :], shift, shift, ALU.logical_shift_right,
                                    ALU.logical_shift_left))
            me.link(v.tensor_copy(total[:, :], whole[:, :]))
            me.link(v.tensor_tensor_scan(block_end[:, :], zeros[:, :], total[:, :], 0.0, ALU.add, ALU.add))
            me.link(v.tensor_tensor(start[:, 0, :], block_end[:, :], total[:, :], ALU.subtract))
            for t in range(1, STREAMS):
                ins = v.tensor_tensor(start[:, t, :], start[:, t - 1, :], count[:, t - 1, :], ALU.add)
                if t < STREAMS - 1:
                    me.link(ins)
            ins.then_inc(start_ready, 1)
            v.wait_ge(end_turned, 1)
            me.link(v.tensor_scalar(end_col[:, :], col[:, 0:1], 1.0 / GROUP, None, ALU.mult))
            v.tensor_scalar(past_end[:, :], group_iota[:, :], end_col[:, 0:1], None, ALU.is_ge)\
                .then_inc(past_ready, 1)
            v.wait_ge(groups_summed, 1)
            for k in range(3):
                w = min(512, gmax - 512 * k)
                v.tensor_scalar(groups_keep[:, 1 + 512 * k:1 + 512 * k + w], sums[k][:, 0:w], float(P - 1), None,
                                ALU.min)
            me.link(v.memset(groups_keep[:, 0:1], 0))
            me.link(v.tensor_scalar(whole[:, 0:1], block_end[:, P - 1:P], 1.0 / GROUP, float(QUAD - 1),
                                    ALU.mult, ALU.add))
            me.link(v.tensor_single_scalar(whole[:, 0:1], whole[:, 0:1], QUAD.bit_length() - 1,
                                           ALU.logical_shift_right))
            me.link(v.tensor_single_scalar(groups_keep[:, gmax + 1:gmax + 2], whole[:, 0:1], 1, ALU.max))

            second = me.n

            def slots_of(i, h, store, store_turn):
                for d in range(2):
                    me.link(v.tensor_copy(hub_key[:, h, d, :].rearrange("p (a b) -> p a b", a=HALF),
                                          hub_keys[d][:, bass.ds((2 * i + h) * HALF, HALF), :]))
                build((2 * i + h) * HALF, h)
                left = [(d, t) for t in range(CHUNKS) for d in range(2)]
                for step in range(HALF):
                    for k in range(2):
                        n = (h * HALF + step) * 2 + k
                        for d, t in left[n % 4 * 8:n % 4 * 8 + 8]:
                            ins = v.tensor_scalar(hub_oh[:, h, d, t, :], iota_b[:, :], hub_key[:, h, d, t:t + 1],
                                                  None, ALU.is_equal)
                        if n % 4 == 3:
                            ins.then_inc(hub_ready, 1)
                        v.wait_ge(ranked, i * 8 + n + 1)
                        for q in range(BK):
                            t = step * STREAMS + BK * k + q
                            ins = v.tensor_tensor_reduce(
                                out=scrap[:, t, :], in0=ranks[k][:, P * q:P * q + P],
                                in1=onehot[:, h, step, BK * k + q, :], scale=1.0, scalar=0.0,
                                op0=ALU.mult, op1=ALU.add, accum_out=slot_f[:, h, t:t + 1])
                        ins.then_inc(extracted, 1)
                me.link(v.tensor_scalar(dropped[:, h, :], keycol[:, h, :], float(blocks), float(1 << 22),
                                        ALU.is_ge, ALU.mult))
                v.wait_ge(extracted, i * 8 + (h + 1) * 4)
                at = bass.ds((2 * store_turn + h) * CHUNKS, CHUNKS)
                v.tensor_tensor(store[0][:, at], slot_f[:, h, :], dropped[:, h, :], ALU.add)\
                    .then_inc(slots_ready, 1)
                v.tensor_copy(store[1][:, at].rearrange("p (a b) -> p a b", a=HALF),
                              values[:, bass.ds((2 * i + h) * HALF, HALF), :]).then_inc(slots_ready, 1)

            with v.Fori(0, EARLY) as i:
                me.base, me.n = second + i * 8, 0
                for h in range(2):
                    slots_of(i, h, early, i)
                assert me.n == 8, me.n
            with v.Fori(0, iters - EARLY) as i:
                me.base, me.n = second + EARLY * 8 + i * 8, 0
                for h in range(2):
                    slots_of(i + EARLY, h, late, i)
            v.wait_ge(hub_counted, iters)
            v.tensor_copy(hub_keep[:, :], hubs[:, 0:P])


def rsqrt(me, v, x, work, y):
    me.link(v.tensor_single_scalar(work.bitcast(I32), x.bitcast(I32), 1, ALU.logical_shift_right))
    me.link(v.tensor_scalar(y.bitcast(I32), work.bitcast(I32), -1.0, float(0x5F3759DF), ALU.mult, ALU.add))
    for _ in range(3):
        me.link(v.tensor_tensor(work, y, y, ALU.mult))
        me.link(v.scalar_tensor_tensor(out=work, in0=work, scalar=-0.5, in1=x, op0=ALU.mult, op1=ALU.mult))
        me.link(v.scalar_tensor_tensor(out=y, in0=work, scalar=1.5, in1=y, op0=ALU.add, op1=ALU.mult))


def norm_rows(v, me, turn, src, stats, mv, rstd, out):
    v.sem_inc(turn, 1)
    for j in range(TB):
        me.mark(v.bn_stats(stats[:, j, :], src[j]))
    me.wait()
    v.sem_inc(turn, 1)
    for j in range(TB):
        me.mark(v.bn_aggr(mv[:, j, 0:2], stats[:, j, :]))
    me.wait()
    me.link(v.tensor_scalar(mv[:, :, 2], mv[:, :, 1], LN_EPS, None, ALU.add))
    rsqrt(me, v, mv[:, :, 2], mv[:, :, 3], rstd[:, :])
    for j in range(TB):
        ins = v.tensor_scalar(out[:, j, :], src[j], mv[:, j, 0:1], rstd[:, j:j + 1], ALU.subtract, ALU.mult)
    return ins


def gin_layer(nc, x, adj, w, keep, late, sorted_edges):
    tiles = x.shape[0]
    groups = tiles // TB
    H = w["W1"].shape[1]
    HK = H // P
    x_keep, xt_keep, proj_keep = keep["x"], keep["xt"], keep["h"]
    with Scope(nc, "gin") as s:
        ident = s.sb("ident", [P, P])
        adj_sb = s.sb("adj", [P, 2, TB, P])
        adj_t = s.sb("adj_t", [P, TB, P])
        xn = s.sb("xn", [P, TB, P])
        agg_t = s.sb("agg_t", [P, TB, P])
        hb = s.sb("hb", [P, TB, H])
        slot_now = s.sb("slot_now", [P, 2, CHUNKS], I32)
        value_now = s.sb("value_now", [P, 2, CHUNKS], I32)
        sq = s.sb("sq", [P, TB, H], BF16)
        ht = s.sb("ht", [P, 2, H])
        xt = s.sb("xt", [P, TB, P])
        stats = s.sb("stats", [P, TB, 6])
        mv = s.sb("mv", [P, TB, 4])
        rstd = s.sb("rstd", [P, TB])
        ss = s.sb("ss", [P, TB])
        rms = s.sb("rms", [P, TB])
        rin = s.sb("rin", [P, 2, TB])
        eps_col = s.sb("eps_col", [P, 1])
        w1 = s.sb("w1", [P, H])
        w2 = s.sb("w2", [P, HK, P])
        b1 = s.sb("b1", [P, H])
        rw = s.sb("rw", [P, H])
        b2 = s.sb("b2", [P, P])
        wg = s.sb("wg", [P, HC])
        b_h = [s.bank(f"b_h{k}") for k in range(TB)]
        b_ht = [s.bank(f"b_ht{k}") for k in range(2)]
        b_adj = b_agg = b_xt = s.bank("b_turn")
        b_o = b_p = s.bank("b_o")

        weights = s.sem("weights")
        consts = s.sem("consts")
        own = s.sem("own")
        turn = s.sem("turn")
        arrived = [s.sem(f"arrived{k}") for k in range(2)]
        adj_turned = s.sem("adj_turned")
        adj_ready = s.sem("adj_ready")
        xn_ready = s.sem("xn_ready")
        agg_done = s.sem("agg_done")
        agg_ready = s.sem("agg_ready")
        h_done = s.sem("h_done")
        hb_ready = s.sem("hb_ready")
        squared = s.sem("squared")
        hn_ready = s.sem("hn_ready")
        silu_ready = s.sem("silu_ready")
        h_turned = s.sem("h_turned")
        ht_ready = s.sem("ht_ready")
        out_done = s.sem("out_done")
        norm_ready = s.sem("norm_ready")
        x_turned = s.sem("x_turned")
        xt_ready = s.sem("xt_ready")
        xt_kept = s.sem("xt_kept")
        proj_done = s.sem("proj_done")
        proj_kept = s.sem("proj_kept")
        staged = s.sem("staged")
        turn_p = s.sem("turn_p")
        scattered = [s.sem(f"scattered{h}") for h in range(2)]
        block = s.block()

        xv = x.rearrange("t n d -> n t d")
        av = adj.rearrange("t n m -> n t m")
        PG = 2 * TB

        @block.sync
        def _(sp):
            for dst, src in ((w1[:, :], w["W1"]), (w2[:, :, :], w["W2"].rearrange("(k p) d -> p k d", p=P)),
                             (b1[:, :], rows_of(w["b1"], H)), (rw[:, :], rows_of(w["rms"], H)),
                             (b2[:, :], rows_of(w["b2"], P)), (wg[:, :], w["W_gat"]),
                             (eps_col[:, :], rows_of(w["eps"], 1))):
                sp.dma_start(dst, src).then_inc(weights, 16)

            def load(t0, k):
                sp.dma_start(adj_sb[:, k, :, :], av[:, bass.ds(t0, TB), :]).then_inc(arrived[k], 16)
                sp.dma_start(x_keep[:, bass.ds(t0, TB), :], xv[:, bass.ds(t0, TB), :]).then_inc(arrived[k], 16)

            for k in range(2):
                load(k * TB, k)
            with sp.Fori(0, groups // 2 - 1) as i:
                for k in range(2):
                    sp.wait_ge(adj_turned, 2 * i + k + 1)
                    load(PG * i + PG + k * TB, k)

        @block.gpsimd
        def _(pool):
            pool.memset(ident[:, :], 0.0).then_inc(consts, 1)
            pool.wait_ge(consts, 1)
            pool.affine_select(out=ident[:, :], in_=ident[:, :], compare_op=ALU.not_equal, fill=1.0,
                               base=0, pattern=[[-1, P]], channel_multiplier=1).then_inc(consts, 1)
            scatter_turns(pool, late[0].shape[1] // (2 * CHUNKS), late[0], late[1], slot_now, value_now, staged,
                          turn_p, scattered, sorted_edges, None)

        @block.tensor
        def _(pe):
            pe.wait_ge(weights, 16 * 7)
            pe.wait_ge(consts, 2)
            with pe.Fori(0, groups // 2) as i:
                for k in range(2):
                    g = 2 * i + k
                    pe.wait_ge(arrived[k], 32 * i + 32)
                    for j in range(TB):
                        mm = pe.transpose(b_adj[:, P * j:P * j + P], adj_sb[:, k, j, :], ident[:, :])
                    mm.then_inc(adj_turned, 1)
                    pe.wait_ge(adj_ready, g + 1)
                    pe.wait_ge(xn_ready, g + 1)
                    for j in range(TB):
                        mm = pe.matmul(b_agg[:, P * j:P * j + P], xn[:, j, :], adj_t[:, j, :],
                                       start=True, stop=True)
                    mm.then_inc(agg_done, 1)
                    pe.wait_ge(agg_ready, g + 1)

                    for j in range(TB):
                        pe.matmul(b_h[j][:, :], agg_t[:, j, :], w1[:, :], start=True, stop=True).then_inc(h_done, 1)

                    def turn_hidden(j):
                        pe.wait_ge(silu_ready, g * TB + j + 1)
                        if j > 1:
                            pe.wait_ge(ht_ready, g * TB + j - 1)
                        for c in range(HK):
                            mm = pe.transpose(b_ht[j % 2][:, P * c:P * c + P], hb[:, j, P * c:P * c + P],
                                              ident[:, :])
                        mm.then_inc(h_turned, 1)

                    turn_hidden(0)
                    for j in range(TB):
                        if j + 1 < TB:
                            turn_hidden(j + 1)
                        pe.wait_ge(ht_ready, g * TB + j + 1)
                        for c in range(HK):
                            mm = pe.matmul(b_o[:, P * j:P * j + P], ht[:, j % 2, P * c:P * c + P], w2[:, c, :],
                                           start=(c == 0), stop=(c == HK - 1))
                        mm.then_inc(out_done, 1)
                    pe.wait_ge(norm_ready, g + 1)
                    for j in range(TB):
                        mm = pe.transpose(b_xt[:, P * j:P * j + P], xn[:, j, :], ident[:, :])
                    mm.then_inc(x_turned, 1)
                    pe.wait_ge(xt_kept, g + 1)
                    for j in range(TB):
                        mm = pe.matmul(b_p[:, HC * j:HC * j + HC], xt[:, j, :], wg[:, :], start=True, stop=True)
                    mm.then_inc(proj_done, 1)

        @block.scalar
        def _(act):
            act.wait_ge(weights, 16 * 7)
            with act.Fori(0, groups) as g:
                act.wait_ge(agg_done, g + 1)
                act.activation(flat(agg_t[:, :, :]), b_agg[:, :], ACT.Copy).then_inc(agg_ready, 1)
                for j in range(TB):
                    act.wait_ge(hb_ready, g * TB + j + 1)
                    act.activation(sq[:, j, :], hb[:, j, :], ACT.Square, accum_out=ss[:, j:j + 1])\
                        .then_inc(squared, 1)
                for j in range(TB):
                    act.wait_ge(hn_ready, g * TB + j + 1)
                    act.activation(hb[:, j, :], hb[:, j, :], ACT.Silu).then_inc(silu_ready, 1)
                act.wait_ge(x_turned, g + 1)
                act.activation(flat(xt[:, :, :]), b_xt[:, :], ACT.Copy).then_inc(xt_ready, 1)
                act.activation(flat(xt_keep[:, bass.ds(g * TB, TB), :]), b_xt[:, :], ACT.Copy).then_inc(xt_kept, 1)

        @block.vector
        def _(v):
            me = Done(v, own)
            v.wait_ge(weights, 16 * 7)
            v.wait_ge(consts, 2)
            per = 54
            with v.Fori(0, groups // 2) as i:
                for k in range(2):
                    g = 2 * i + k
                    me.base, me.n = per * g, 0
                    src = x_keep[:, bass.ds(g * TB, TB), :]
                    v.wait_ge(arrived[k], 32 * i + 32)
                    norm_rows(v, me, turn, [src[:, j, :] for j in range(TB)], stats, mv, rstd, xn).then_inc(xn_ready, 1)
                    v.wait_ge(adj_turned, g + 1)
                    v.scalar_tensor_tensor(
                        out=adj_t[:, :, :], in0=over(ident[:, :].unsqueeze(1), [P, TB, P]),
                        scalar=eps_col[:, 0:1], in1=b_adj[:, :].rearrange("p (a b) -> p a b", a=TB),
                        op0=ALU.mult, op1=ALU.add).then_inc(adj_ready, 1)

                    for j in range(TB):
                        v.wait_ge(h_done, g * TB + j + 1)
                        v.tensor_tensor(hb[:, j, :], b_h[j][:, :], b1[:, :], ALU.add).then_inc(hb_ready, 1)
                    me.link(v.tensor_tensor(src, src, over(b2[:, :].unsqueeze(1), [P, TB, P]), ALU.add))
                    v.wait_ge(squared, g * TB + TB)
                    me.link(v.tensor_scalar(rin[:, 0, :], ss[:, :], 1.0 / H, RMS_EPS, ALU.mult, ALU.add))
                    rsqrt(me, v, rin[:, 0, :], rin[:, 1, :], rms[:, :])
                    for j in range(TB):
                        v.scalar_tensor_tensor(out=hb[:, j, :], in0=hb[:, j, :], scalar=rms[:, j:j + 1],
                                               in1=rw[:, :], op0=ALU.mult, op1=ALU.mult).then_inc(hn_ready, 1)
                    for j in range(TB):
                        v.wait_ge(h_turned, g * TB + j + 1)
                        if j > 1:
                            v.wait_ge(out_done, g * TB + j - 1)
                        v.tensor_copy(ht[:, j % 2, :], b_ht[j % 2][:, :]).then_inc(ht_ready, 1)
                    v.wait_ge(out_done, g * TB + TB)
                    me.link(v.tensor_tensor(src, src, b_o[:, :].rearrange("p (a b) -> p a b", a=TB), ALU.add))
                    norm_rows(v, me, turn, [src[:, j, :] for j in range(TB)], stats, mv, rstd, xn)\
                        .then_inc(norm_ready, 1)
                    v.wait_ge(proj_done, g + 1)
                    v.tensor_copy(proj_keep[:, bass.ds(g * TB, TB), 0:HC],
                                  b_p[:, 0:TB * HC].rearrange("p (a b) -> p a b", a=TB)).then_inc(proj_kept, 1)
                    n = me.n
            assert n == per, n


def edge_attention(nc, w, sorted_edges, table, keep):
    tiles = keep["x"].shape[1]
    nodes = tiles * P
    hk, dst_keep, acc, groups_keep, gates = keep["h"], keep["dst"], keep["acc"], keep["groups"], keep["gates"]
    last = groups_keep.shape[1] - 1
    E = CH
    with Scope(nc, "att") as s:
        ident = s.sb("ident", [P, P])
        iota_f = s.sb("iota_f", [P, P])
        att_src = s.sb("att_src", [P, HC])
        att_dst = s.sb("att_dst", [P, HC])
        b_gat = s.sb("b_gat", [P, HC])
        gamma = s.sb("gamma", [P, HC])
        beta = s.sb("beta", [P, HC])
        prod = s.sb("prod", [P, tiles, HC])
        self_e = s.sb("self_e", [P, tiles, HEADS])
        hub_e = s.sb("hub_e", [P, tiles, HEADS])
        hub_row = s.sb("hub_row", [P, ROW])
        work = s.sb("work", [P, tiles, 2])
        small = s.sb("small", [P, tiles])
        small2 = s.sb("small2", [P, tiles])
        rs = s.sb("rs", [P, tiles])
        top = s.sb("top", [P, HEADS])
        gmax_sb = s.sb("gmax", [P, HEADS])
        rows = s.sb("rows", [P, QUAD, GC], I32)
        idx = s.sb("idx", [P, QUAD, GC], I32)
        low = s.sb("low", [P, QUAD, GC])
        got = s.sb("got", [P, QUAD, GC, ROW])
        oh = s.sb("oh", [P, QUAD, GC, P])
        oht = s.sb("oht", [P, GC, P])
        dst_blk = s.sb("dst_blk", [P, 2, 2 * HEADS])
        e_a = s.sb("e_a", [P, GC, HEADS])
        msg = s.sb("msg", [P, 2, GC, ROW])
        scores = s.sb("scores", [P, tiles, E])
        pick = [s.sb(f"pick{k}", [P, tiles, E]) for k in range(2)]
        b_t = s.bank("b_t")
        b_d = [s.bank(f"b_d{k}") for k in range(2)]
        b_s = [s.bank(f"b_s{k}") for k in range(2)]

        weights = s.sem("weights")
        consts = s.sem("consts")
        own = s.sem("own")
        table_ready = s.sem("table_ready")
        table_out = s.sem("table_out")
        top_ready = s.sem("top_ready")
        top_all = s.sem("top_all")
        self_ready = s.sem("self_ready")
        self_exp = s.sem("self_exp")
        rows_in = [s.sem(f"rows_in{k}") for k in range(QUAD)]
        idx_ready = s.sem("idx_ready")
        turn = s.sem("turn")
        gathered = [s.sem(f"gathered{k}") for k in range(QUAD)]
        oh_ready = s.sem("oh_ready")
        oh_turned = s.sem("oh_turned")
        oht_ready = s.sem("oht_ready")
        dst_done = s.sem("dst_done")
        e_ready = s.sem("e_ready")
        ee_ready = s.sem("ee_ready")
        msg_ready = s.sem("msg_ready")
        sum_done = s.sem("sum_done")
        diff_ready = s.sem("diff_ready")
        diff_exp = s.sem("diff_exp")
        zero_ready = s.sem("zero_ready")
        hub_in = s.sem("hub_in")
        hub_scores = s.sem("hub_scores")
        hub_exp = s.sem("hub_exp")
        block = s.block()

        slots_view = sorted_edges.rearrange("(g p c) o -> g p (c o)", p=P, c=GC)

        def quads_of(eng):
            return eng.value_load(groups_keep[0:1, last:last + 1], min_val=1, max_val=(last - 1 - SPARE) // QUAD)

        @block.sync
        def _(sp):
            for dst, src, n in ((att_src, "att_src", HC), (att_dst, "att_dst", HC), (b_gat, "b_gat", HC),
                                (gamma, "ln_gamma", HC), (beta, "ln_beta", HC)):
                sp.dma_start(dst[:, :], rows_of(w[src], n)).then_inc(weights, 16)
            for k in range(QUAD):
                sp.dma_start(rows[:, k, :], slots_view[k]).then_inc(rows_in[k], 16)
            sp.wait_ge(table_ready, 1)
            sp.dma_start(table.rearrange("(t n) f -> n t f", n=P), hk[:, :, :]).then_inc(table_out, 16)
            sp.wait_ge(table_out, 16)
            sp.dma_start(hub_row[:, :], table[nodes - 1:nodes, :].broadcast_to([P, ROW])).then_inc(hub_in, 16)
            n = quads_of(sp)
            with sp.Fori(0, n) as i:
                for k in range(QUAD):
                    sp.wait_ge(idx_ready, QUAD * i + k + 1)
                    sp.dma_start(rows[:, k, :],
                                 slots_view[bass.ds(QUAD * i + QUAD + k, 1)].rearrange("g p c -> p (g c)"))\
                        .then_inc(rows_in[k], 16)
            sp.wait_ge(table_out, 16)
            for k in range(QUAD):
                sp.wait_ge(rows_in[k], 16 * n + 16)
                sp.sem_inc(turn, 1)

        @block.gpsimd
        def _(pool):
            pool.memset(ident[:, :], 0.0).then_inc(consts, 1)
            pool.wait_ge(consts, 1)
            pool.affine_select(out=ident[:, :], in_=ident[:, :], compare_op=ALU.not_equal, fill=1.0,
                               base=0, pattern=[[-1, P]], channel_multiplier=1).then_inc(consts, 1)
            pool.iota(iota_f[:, :], [[1, P]], base=0, channel_multiplier=0,
                      allow_small_or_imprecise_dtypes=True).then_inc(consts, 1)
            pool.wait_ge(top_ready, 1)
            pool.partition_all_reduce(gmax_sb[:, :], top[:, :], P, bass.bass_isa.ReduceOp.max).then_inc(top_all, 1)
            pool.wait_ge(table_out, 16)

            def gather(g, k):
                pool.wait_ge(idx_ready, g + 1)
                pool.sem_inc(turn, 1)
                for c in range(GC):
                    pool.indirect_dma_start(
                        out=got[:, k, c, :], out_offset=None, in_=table,
                        in_offset=bass.IndirectOffsetOnAxis(ap=idx[:, k, c:c + 1].bitcast(U32), axis=0))\
                        .then_inc(gathered[k], 16)

            for g in range(QUAD - 1):
                gather(g, g)
            n = quads_of(pool)
            with pool.Fori(0, n) as i:
                for k in range(QUAD):
                    gather(QUAD * i + QUAD - 1 + k, (k + QUAD - 1) % QUAD)
            for k in range(QUAD):
                pool.wait_ge(gathered[k], (16 * GC) * n + (16 * GC if k < QUAD - 1 else 0))
                pool.sem_inc(turn, 1)

        @block.tensor
        def _(pe):
            pe.wait_ge(consts, 3)

            def targets(g, k):
                pe.wait_ge(oh_ready, g + 1)
                for c in range(GC):
                    mm = pe.transpose(b_t[:, P * c:P * c + P], oh[:, k, c, :], ident[:, :])
                mm.then_inc(oh_turned, 1)
                pe.wait_ge(oht_ready, g + 1)
                W = 2 * HEADS
                for c in range(GC):
                    mm = pe.matmul(b_d[k % 2][:, W * c:W * c + W], oht[:, c, :], dst_blk[:, k % 2, :],
                                   start=True, stop=True)
                mm.then_inc(dst_done, 1)

            targets(0, 0)
            pe.wait_ge(zero_ready, 1)
            pe.matmul(b_s[1][:, 0:ROW], ident[:, :], msg[:, 1, 0, :], start=True, stop=True).then_inc(sum_done, 1)
            n = quads_of(pe)
            with pe.Fori(0, n) as i:
                for k in range(QUAD):
                    g = QUAD * i + k
                    targets(g + 1, (k + 1) % QUAD)
                    pe.wait_ge(msg_ready, g + 1)
                    for c in range(GC):
                        mm = pe.matmul(b_s[k % 2][:, 0:ROW], oh[:, k, c, :], msg[:, k % 2, c, :],
                                       start=(c == 0), stop=(c == GC - 1))
                    mm.then_inc(sum_done, 1)

        @block.scalar
        def _(act):
            act.wait_ge(self_ready, 1)
            act.activation(self_e[:, :, :], self_e[:, :, :], ACT.Exp).then_inc(self_exp, 1)
            act.wait_ge(hub_scores, 1)
            act.activation(hub_e[:, :, :], hub_e[:, :, :], ACT.Exp).then_inc(hub_exp, 1)

            def turned(g):
                act.wait_ge(oh_turned, g + 1)
                act.activation(flat(oht[:, :, :]), b_t[:, :], ACT.Copy).then_inc(oht_ready, 1)

            turned(0)
            n = quads_of(act)
            with act.Fori(0, n) as i:
                for k in range(QUAD):
                    g = QUAD * i + k
                    turned(g + 1)
                    act.wait_ge(e_ready, g + 1)
                    act.activation(msg[:, k % 2, :, HC:ROW], e_a[:, :, :], ACT.Exp).then_inc(ee_ready, 1)
            act.wait_ge(diff_ready, 1)
            act.activation(small2[:, :], small2[:, :], ACT.Exp).then_inc(diff_exp, 1)

        @block.vector
        def _(v):
            me = Done(v, own)
            v.wait_ge(weights, 16 * 5)
            v.wait_ge(consts, 3)
            h = hk[:, :, 0:HC]
            T3 = [P, tiles, HC]
            me.link(v.tensor_tensor(prod[:, :, :], h, over(att_src[:, :].unsqueeze(1), T3), ALU.mult))
            me.link(v.tensor_reduce(hk[:, :, HC:ROW], prod[:, :, :].rearrange("p t (h c) -> p t h c", c=CH),
                                    AX.X, ALU.add))
            me.link(v.tensor_tensor(prod[:, :, :], h, over(att_dst[:, :].unsqueeze(1), T3), ALU.mult))
            tgt, bound = dst_keep[:, :, 0:HEADS], dst_keep[:, :, HEADS:2 * HEADS]
            v.tensor_reduce(tgt, prod[:, :, :].rearrange("p t (h c) -> p t h c", c=CH),
                            AX.X, ALU.add).then_inc(table_ready, 1)
            v.wait_ge(table_ready, 1)
            v.tensor_reduce(top[:, :], hk[:, :, HC:ROW].rearrange("p t h -> p h t"), AX.X, ALU.max)\
                .then_inc(top_ready, 1)
            v.memset(msg[:, 1, 0, :], 0.0).then_inc(zero_ready, 1)
            v.wait_ge(top_all, 1)
            top_b = over(gmax_sb[:, :].unsqueeze(1), [P, tiles, HEADS])
            me.link(v.tensor_tensor(bound, tgt, top_b, ALU.add))
            me.link(v.scalar_tensor_tensor(out=bound, in0=bound, scalar=SLOPE, in1=bound, op0=ALU.mult, op1=ALU.max))
            me.link(v.tensor_tensor(self_e[:, :, :], hk[:, :, HC:ROW], tgt, ALU.add))
            me.link(v.scalar_tensor_tensor(out=self_e[:, :, :], in0=self_e[:, :, :], scalar=SLOPE,
                                           in1=self_e[:, :, :], op0=ALU.mult, op1=ALU.max))
            v.tensor_tensor(self_e[:, :, :], self_e[:, :, :], bound, ALU.subtract).then_inc(self_ready, 1)
            v.wait_ge(self_exp, 1)
            me.link(v.tensor_copy(acc[:, :, HC:ROW], self_e[:, :, :]))
            me.link(v.tensor_tensor(acc[:, :, 0:HC].rearrange("p t (h c) -> p t h c", c=CH),
                                    hk[:, :, 0:HC].rearrange("p t (h c) -> p t h c", c=CH),
                                    over(self_e[:, :, :].unsqueeze(3), [P, tiles, HEADS, CH]), ALU.mult))

            v.wait_ge(hub_in, 16)
            T2 = [P, tiles, HEADS]
            me.link(v.tensor_tensor(hub_e[:, :, :], tgt, over(hub_row[:, HC:ROW].unsqueeze(1), T2), ALU.add))
            me.link(v.scalar_tensor_tensor(out=hub_e[:, :, :], in0=hub_e[:, :, :], scalar=SLOPE,
                                           in1=hub_e[:, :, :], op0=ALU.mult, op1=ALU.max))
            v.tensor_tensor(hub_e[:, :, :], hub_e[:, :, :], bound, ALU.subtract).then_inc(hub_scores, 1)
            v.wait_ge(hub_exp, 1)
            me.link(v.tensor_tensor(hub_e[:, :, :], hub_e[:, :, :], over(keep["hub"][:, :].unsqueeze(2), T2), ALU.mult))
            me.link(v.tensor_tensor(acc[:, :, HC:ROW], acc[:, :, HC:ROW], hub_e[:, :, :], ALU.add))
            for q in range(HEADS):
                part = prod[:, :, CH * q:CH * q + CH]
                me.link(v.tensor_tensor(part, over(hub_e[:, :, q:q + 1], [P, tiles, CH]),
                                        over(hub_row[:, CH * q:CH * q + CH].unsqueeze(1), [P, tiles, CH]), ALU.mult))
            me.link(v.tensor_tensor(acc[:, :, 0:HC], acc[:, :, 0:HC], prod[:, :, :], ALU.add))

            def indices(turns, k):
                v.wait_ge(rows_in[k], 16 * turns)
                me.link(v.tensor_scalar(idx[:, k, :], rows[:, k, :], 7, nodes - 1, ALU.logical_shift_right,
                                        ALU.bitwise_and))
                v.scalar_tensor_tensor(out=low[:, k, :], in0=idx[:, k, :], scalar=-float(P), in1=rows[:, k, :],
                                       op0=ALU.mult, op1=ALU.add).then_inc(idx_ready, 1)

            def block_at(col):
                return v.value_load(groups_keep[0:1, bass.ds(col, 1)], min_val=0, max_val=tiles - 1)

            def onehots(g, k):
                blk = block_at(g + 1)
                v.tensor_copy(dst_blk[:, k % 2, :], dst_keep[:, bass.ds(blk, 1), :].rearrange("p a h -> p (a h)"))
                for c in range(GC):
                    ins = v.tensor_scalar(oh[:, k, c, :], iota_f[:, :], low[:, k, c:c + 1], None, ALU.is_equal)
                ins.then_inc(oh_ready, 1)

            def add_sum(g, k):
                blk = block_at(g + 1)
                v.wait_ge(sum_done, g + 2)
                here = acc[:, bass.ds(blk, 1), :].rearrange("p a f -> p (a f)")
                me.link(v.tensor_tensor(here, here, b_s[k % 2][:, 0:ROW], ALU.add))

            def messages(i, k):
                g = QUAD * i + k
                v.wait_ge(dst_done, g + 1)
                v.wait_ge(gathered[k], (16 * GC) * i + 16 * GC)
                per_edge = b_d[k % 2][:, 0:GC * 2 * HEADS].rearrange("p (c h) -> p c h", h=2 * HEADS)
                me.link(v.tensor_tensor(e_a[:, :, :], got[:, k, :, HC:ROW], per_edge[:, :, 0:HEADS], ALU.add))
                me.link(v.scalar_tensor_tensor(out=e_a[:, :, :], in0=e_a[:, :, :], scalar=SLOPE, in1=e_a[:, :, :],
                                               op0=ALU.mult, op1=ALU.max))
                v.tensor_tensor(e_a[:, :, :], e_a[:, :, :], per_edge[:, :, HEADS:2 * HEADS], ALU.subtract)\
                    .then_inc(e_ready, 1)
                add_sum(g - 1, k - 1)
                v.wait_ge(ee_ready, g + 1)
                v.tensor_tensor(msg[:, k % 2, :, 0:HC].rearrange("p c (h f) -> p c h f", f=CH),
                                got[:, k, :, 0:HC].rearrange("p c (h f) -> p c h f", f=CH),
                                over(msg[:, k % 2, :, HC:ROW].unsqueeze(3), [P, GC, HEADS, CH]), ALU.mult)\
                    .then_inc(msg_ready, 1)

            for k in range(QUAD - 1):
                indices(1, k)
            v.wait_ge(idx_ready, QUAD - 1)
            onehots(0, 0)
            first = me.n
            per = QUAD * 4
            n = quads_of(v)
            with v.Fori(0, n) as i:
                me.base, me.n = first + per * i, 0
                for k in range(QUAD):
                    indices(i + 1 + (k > 0), (k + QUAD - 1) % QUAD)
                    onehots(QUAD * i + k + 1, (k + 1) % QUAD)
                    messages(i, k)
                assert me.n == per, me.n
            me.base, me.n = first + per * n, 0
            add_sum(QUAD * n - 1, QUAD - 1)
            fin = Done(v, s.sem("own2"))
            acc_h = acc[:, :, 0:HC].rearrange("p t (h c) -> p t h c", c=CH)
            fin.link(v.tensor_scalar(acc[:, :, HC:ROW], acc[:, :, HC:ROW], 1e-16, None, ALU.add))
            fin.link(v.reciprocal(self_e[:, :, :], acc[:, :, HC:ROW]))
            fin.link(v.tensor_tensor(prod[:, :, :].rearrange("p t (h c) -> p t h c", c=CH), acc_h,
                                     over(self_e[:, :, :].unsqueeze(3), [P, tiles, HEADS, CH]), ALU.mult))
            fin.link(v.tensor_tensor(prod[:, :, :], prod[:, :, :], over(b_gat[:, :].unsqueeze(1), T3), ALU.add))
            fin.link(v.tensor_reduce(small[:, :], prod[:, :, :], AX.X, ALU.add))
            fin.link(v.tensor_scalar(small[:, :], small[:, :], 1.0 / HC, None, ALU.mult))
            fin.link(v.tensor_tensor(prod[:, :, :], prod[:, :, :], over(small[:, :].unsqueeze(2), T3), ALU.subtract))
            sq = acc[:, :, 0:HC]
            fin.link(v.tensor_tensor(sq, prod[:, :, :], prod[:, :, :], ALU.mult))
            fin.link(v.tensor_reduce(small[:, :], sq, AX.X, ALU.add))
            fin.link(v.tensor_scalar(small[:, :], small[:, :], 1.0 / HC, LN_EPS, ALU.mult, ALU.add))
            rsqrt(fin, v, small[:, :], small2[:, :], rs[:, :])
            fin.link(v.tensor_tensor(prod[:, :, :], prod[:, :, :], over(rs[:, :].unsqueeze(2), T3), ALU.mult))
            fin.link(v.tensor_tensor(prod[:, :, :], prod[:, :, :], over(gamma[:, :].unsqueeze(1), T3), ALU.mult))
            fin.link(v.tensor_tensor(prod[:, :, :], prod[:, :, :], over(beta[:, :].unsqueeze(1), T3), ALU.add))
            fin.link(v.tensor_reduce(scores[:, :, :], prod[:, :, :].rearrange("p t (h c) -> p t c h", c=CH),
                                     AX.X, ALU.add))
            fin.link(v.tensor_scalar(scores[:, :, :], scores[:, :, :], 1.0 / HEADS, None, ALU.mult))
            top_two(v, fin, scores, pick, small, small2, work)
            v.tensor_tensor(small2[:, :], small2[:, :], small[:, :], ALU.subtract).then_inc(diff_ready, 1)
            v.wait_ge(diff_exp, 1)
            fin.link(v.tensor_scalar(small[:, :], small2[:, :], 1.0, None, ALU.add))
            fin.link(v.reciprocal(small[:, :], small[:, :]))
            fin.link(v.tensor_tensor(small2[:, :], small2[:, :], small[:, :], ALU.mult))
            T4 = [P, tiles, E]
            fin.link(v.tensor_tensor(pick[0][:, :, :], pick[0][:, :, :], over(small[:, :].unsqueeze(2), T4), ALU.mult))
            fin.link(v.tensor_tensor(pick[1][:, :, :], pick[1][:, :, :], over(small2[:, :].unsqueeze(2), T4), ALU.mult))
            fin.link(v.tensor_tensor(gates[:, :, 0:E], pick[0][:, :, :], pick[1][:, :, :], ALU.add))


def top_two(v, me, scores, pick, first, second, work):
    E = scores.shape[2]
    tiles = scores.shape[1]
    BIG = 3.0e38
    found, eq, = work[:, :, 0], work[:, :, 1]
    for r, (mask, best) in enumerate(((pick[0], first), (pick[1], second))):
        src = scores if r == 0 else pick[1]
        me.link(v.tensor_reduce(best[:, :], src[:, :, :], AX.X, ALU.max))
        me.link(v.memset(found, 0.0))
        for e in range(E):
            me.link(v.tensor_tensor(eq, src[:, :, e], best[:, :], ALU.is_equal))
            me.link(v.tensor_tensor(mask[:, :, e], eq, found, ALU.is_gt))
            me.link(v.tensor_tensor(found, found, eq, ALU.max))
        if r == 0:
            me.link(v.scalar_tensor_tensor(out=pick[1][:, :, :], in0=pick[0][:, :, :], scalar=-BIG,
                                           in1=scores[:, :, :], op0=ALU.mult, op1=ALU.add))


def dense_attention(nc, adj, w, keep):
    x_keep, xt_keep, logits_keep = keep["x"], keep["xt"], keep["logits"]
    tiles = x_keep.shape[1]
    groups = tiles // TB
    E = w["gate_w"].shape[1]
    with Scope(nc, "gat") as s:
        ident = s.sb("ident", [P, P])
        adj_sb = s.sb("adj", [P, 2, TB, P])
        xn = s.sb("xn", [P, TB, P])
        xt = s.sb("xt", [P, TB, P])
        h = s.sb("h", [P, TB, P])
        ha = s.sb("ha", [P, TB, P])
        lg = s.sb("lg", [P, TB, P])
        off = s.sb("off", [P, TB, P])
        att = s.sb("att", [P, TB, P])
        att_t = s.sb("att_t", [P, TB, P])
        hp = s.sb("hp", [P, TB, P])
        hm = s.sb("hm", [P, TB, P])
        stats = s.sb("stats", [P, TB, 6])
        mv = s.sb("mv", [P, TB, 4])
        rstd = s.sb("rstd", [P, TB])
        sc = s.sb("sc", [P, TB])
        sc2 = s.sb("sc2", [P, TB])
        negmax = s.sb("negmax", [P, TB])
        den = s.sb("den", [P, TB])
        rden = s.sb("rden", [P, TB])
        wh = s.sb("wh", [P, P])
        a1 = s.sb("a1", [P, P])
        a2 = s.sb("a2", [P, P])
        gw = s.sb("gw", [P, E])
        gb = s.sb("gb", [P, E])
        b_x = s.bank("b_x")
        b_h = s.bank("b_h")
        b_a = s.bank("b_a")
        b_o = s.bank("b_o")
        b_xt = s.bank("b_xt")
        b_p = s.bank("b_p")
        weights = s.sem("weights")
        consts = s.sem("consts")
        own = s.sem("own")
        turn = s.sem("turn")
        arrived = [s.sem(f"arrived{k}") for k in range(2)]
        adj_used = s.sem("adj_used")
        xn_ready = s.sem("xn_ready")
        xn_turned = s.sem("xn_turned")
        xt_ready = s.sem("xt_ready")
        h_done = s.sem("h_done")
        h_ready = s.sem("h_ready")
        max_ready = s.sem("max_ready")
        att_ready = s.sem("att_ready")
        att_turned = s.sem("att_turned")
        att_t_ready = s.sem("att_t_ready")
        out_done = s.sem("out_done")
        hm_ready = s.sem("hm_ready")
        exp_ready = s.sem("exp_ready")
        norm_ready = s.sem("norm_ready")
        x_turned = s.sem("x_turned")
        xt2_ready = s.sem("xt2_ready")
        xt_kept = s.sem("xt_kept")
        proj_done = s.sem("proj_done")
        proj_kept = s.sem("proj_kept")
        block = s.block()
        av = adj.rearrange("t n m -> n t m")

        @block.sync
        def _(sp):
            for dst, src in ((wh[:, :], w["W"]), (a1[:, :], rows_of(w["a"][0:P, 0], P)),
                             (a2[:, :], rows_of(w["a"][P:2 * P, 0], P)), (gw[:, :], w["gate_w"]),
                             (gb[:, :], rows_of(w["gate_b"], E))):
                sp.dma_start(dst, src).then_inc(weights, 16)
            for k in range(2):
                sp.dma_start(adj_sb[:, k, :, :], av[:, k * TB:k * TB + TB, :]).then_inc(arrived[k], 16)
            with sp.Fori(0, groups // 2 - 1) as i:
                for k in range(2):
                    sp.wait_ge(adj_used, 2 * i + k + 1)
                    sp.dma_start(adj_sb[:, k, :, :], av[:, bass.ds(2 * TB * i + 2 * TB + k * TB, TB), :])\
                        .then_inc(arrived[k], 16)

        @block.gpsimd
        def _(pool):
            pool.memset(ident[:, :], 0.0).then_inc(consts, 1)
            pool.wait_ge(consts, 1)
            pool.affine_select(out=ident[:, :], in_=ident[:, :], compare_op=ALU.not_equal, fill=1.0,
                               base=0, pattern=[[-1, P]], channel_multiplier=1).then_inc(consts, 1)
            with pool.Fori(0, groups) as g:
                pool.wait_ge(xt2_ready, g + 1)
                pool.tensor_copy(xt_keep[:, bass.ds(g * TB, TB), :], xt[:, :, :]).then_inc(xt_kept, 1)

        @block.tensor
        def _(pe):
            pe.wait_ge(weights, 16 * 5)
            pe.wait_ge(consts, 2)
            with pe.Fori(0, groups) as g:
                pe.wait_ge(xn_ready, g + 1)
                for j in range(TB):
                    mm = pe.transpose(b_x[:, P * j:P * j + P], xn[:, j, :], ident[:, :])
                mm.then_inc(xn_turned, 1)
                pe.wait_ge(xt_ready, g + 1)
                for j in range(TB):
                    mm = pe.matmul(b_h[:, P * j:P * j + P], xt[:, j, :], wh[:, :], start=True, stop=True)
                mm.then_inc(h_done, 1)
                pe.wait_ge(att_ready, g + 1)
                for j in range(TB):
                    mm = pe.transpose(b_a[:, P * j:P * j + P], att[:, j, :], ident[:, :])
                mm.then_inc(att_turned, 1)
                pe.wait_ge(att_t_ready, g + 1)
                for j in range(TB):
                    mm = pe.matmul(b_o[:, P * j:P * j + P], att_t[:, j, :], h[:, j, :], start=True, stop=True)
                mm.then_inc(out_done, 1)
                pe.wait_ge(norm_ready, g + 1)
                for j in range(TB):
                    mm = pe.transpose(b_xt[:, P * j:P * j + P], xn[:, j, :], ident[:, :])
                mm.then_inc(x_turned, 1)
                pe.wait_ge(xt2_ready, g + 1)
                for j in range(TB):
                    mm = pe.matmul(b_p[:, E * j:E * j + E], xt[:, j, :], gw[:, :], start=True, stop=True)
                mm.then_inc(proj_done, 1)

        @block.scalar
        def _(act):
            with act.Fori(0, groups) as g:
                act.wait_ge(xn_turned, g + 1)
                act.wait_ge(xt_kept, g + 1)
                act.activation(flat(xt[:, :, :]), b_x[:, :], ACT.Copy).then_inc(xt_ready, 1)
                act.wait_ge(h_done, g + 1)
                act.activation(flat(h[:, :, :]), b_h[:, :], ACT.Copy).then_inc(h_ready, 1)
                act.wait_ge(max_ready, g + 1)
                for j in range(TB):
                    ins = act.activation(att[:, j, :], lg[:, j, :], ACT.Exp, bias=negmax[:, j:j + 1],
                                         accum_out=den[:, j:j + 1])
                ins.then_inc(att_ready, 1)
                act.wait_ge(att_turned, g + 1)
                act.activation(flat(att_t[:, :, :]), b_a[:, :], ACT.Copy).then_inc(att_t_ready, 1)
                act.wait_ge(hm_ready, g + 1)
                act.activation(flat(hm[:, :, :]), flat(hm[:, :, :]), ACT.Exp).then_inc(exp_ready, 1)
                act.wait_ge(x_turned, g + 1)
                act.activation(flat(xt[:, :, :]), b_xt[:, :], ACT.Copy).then_inc(xt2_ready, 1)

        @block.vector
        def _(v):
            me = Done(v, own)
            v.wait_ge(weights, 16 * 5)
            v.wait_ge(consts, 2)
            v.sem_inc(xt_kept, 1)
            me.link(v.tensor_tensor(a1[:, :], a1[:, :], a2[:, :], ALU.add))
            per = 33+22
            T = [P, TB, P]
            with v.Fori(0, groups // 2) as i:
                for k in range(2):
                    g = 2 * i + k
                    me.base, me.n = 1 + per * g, 0
                    src = x_keep[:, bass.ds(g * TB, TB), :]
                    srcs = [src[:, j, :] for j in range(TB)]
                    norm_rows(v, me, turn, srcs, stats, mv, rstd, xn).then_inc(xn_ready, 1)
                    v.wait_ge(h_ready, g + 1)
                    me.link(v.tensor_tensor(ha[:, :, :], h[:, :, :], over(a1[:, :].unsqueeze(1), T), ALU.mult))
                    me.link(v.tensor_reduce(sc[:, :], ha[:, :, :], AX.X, ALU.add))
                    me.link(v.scalar_tensor_tensor(out=sc2[:, :], in0=sc[:, :], scalar=SLOPE, in1=sc[:, :],
                                                   op0=ALU.mult, op1=ALU.max))
                    v.wait_ge(arrived[k], 16 * i + 16)
                    for j in range(TB):
                        me.mark(v.tensor_scalar(lg[:, j, :], adj_sb[:, k, j, :], 0.0, sc2[:, j:j + 1],
                                                ALU.is_gt, ALU.mult))
                    me.mark(v.tensor_scalar(off[:, :, :], adj_sb[:, k, :, :], 0.0, NEG, ALU.is_le, ALU.mult))
                    me.wait()
                    v.tensor_tensor(lg[:, :, :], lg[:, :, :], off[:, :, :], ALU.add).then_inc(adj_used, 1)
                    v.wait_ge(adj_used, g + 1)
                    v.tensor_reduce(negmax[:, :], lg[:, :, :], AX.X, ALU.max, negate=True).then_inc(max_ready, 1)
                    v.wait_ge(att_ready, g + 1)
                    me.link(v.reciprocal(rden[:, :], den[:, :]))
                    v.wait_ge(out_done, g + 1)
                    for j in range(TB):
                        me.mark(v.tensor_scalar(hp[:, j, :], b_o[:, P * j:P * j + P], rden[:, j:j + 1], None,
                                                ALU.mult))
                    me.wait()
                    v.tensor_scalar(hm[:, :, :], hp[:, :, :], 0.0, None, ALU.min).then_inc(hm_ready, 1)
                    me.link(v.scalar_tensor_tensor(out=src, in0=hp[:, :, :], scalar=0.0, in1=src,
                                                   op0=ALU.max, op1=ALU.add))
                    v.wait_ge(exp_ready, g + 1)
                    me.link(v.scalar_tensor_tensor(out=src, in0=hm[:, :, :], scalar=-1.0, in1=src,
                                                   op0=ALU.add, op1=ALU.add))
                    norm_rows(v, me, turn, srcs, stats, mv, rstd, xn).then_inc(norm_ready, 1)
                    v.wait_ge(proj_done, g + 1)
                    v.tensor_tensor(logits_keep[:, bass.ds(g * TB, TB), :],
                                    b_p[:, 0:TB * E].rearrange("p (a b) -> p a b", a=TB),
                                    over(gb[:, :].unsqueeze(1), [P, TB, E]), ALU.add).then_inc(proj_kept, 1)
                    n = me.n
            assert n == per, n


def experts(nc, tag, w, keep, softmax_gates, out):
    W1, b1, W2, b2 = w["W1"], w["b1"], w["W2"], w["b2"]
    E, D, H = W1.shape
    HK = H // P
    x_keep, xt_keep, gates = keep["x"], keep["xt"], keep["gates"]
    tiles = x_keep.shape[1]
    groups = tiles // TB
    N = TB * P
    with Scope(nc, tag) as s:
        ident = s.sb("ident", [P, P])
        w1 = s.sb("w1", [P, E, H])
        w2 = s.sb("w2", [P, E * HK, D])
        b1c = s.sb("b1c", [P, E * HK])
        b2r = s.sb("b2r", [E, D])
        gate = s.sb("gate", [P, TB, E])
        gate_t = s.sb("gate_t", [E, N])
        hid = [s.sb(f"hid{k}", [P, HK, N]) for k in range(2)]
        acc = s.sb("acc", [P, TB, D])
        b_z = [s.bank(f"b_z{k}") for k in range(4)]
        b_y = [s.bank(f"b_y{k}") for k in range(2)]
        b_g = s.bank("b_g")
        b_b = s.bank("b_b")
        weights = s.sem("weights")
        consts = s.sem("consts")
        own = s.sem("own")
        gates_ready = s.sem("gates_ready")
        gate_ready = s.sem("gate_ready")
        gate_turned = s.sem("gate_turned")
        gate_t_ready = s.sem("gate_t_ready")
        bias_done = s.sem("bias_done")
        z_done = s.sem("z_done")
        hid_ready = s.sem("hid_ready")
        y_done = s.sem("y_done")
        y_added = s.sem("y_added")
        stored = s.sem("stored")
        shifted = s.sem("shifted")
        turn = s.sem("turn")
        exped = s.sem("exped")
        block = s.block()

        @block.sync
        def _(sp):
            sp.dma_start(w1[:, :, :], W1.rearrange("e d h -> d e h")).then_inc(weights, 16)
            sp.dma_start(w2[:, :, :], W2.rearrange("e (k p) d -> p (e k) d", p=P)).then_inc(weights, 16)
            sp.dma_start(b1c[:, :], b1.rearrange("e (k p) -> p (e k)", p=P),
                         allow_slow_non_contiguous=True).then_inc(weights, 16)
            sp.dma_start(b2r[:, :], b2).then_inc(weights, 16)
            if out is not None:
                ov = out.rearrange("t n d -> n t d")
                with sp.Fori(0, groups) as g:
                    sp.wait_ge(y_added, g * E + E)
                    sp.dma_start(ov[:, bass.ds(g * TB, TB), :], x_keep[:, bass.ds(g * TB, TB), :])\
                        .then_inc(stored, 16)
                sp.wait_ge(stored, 16 * groups)

        @block.gpsimd
        def _(pool):
            pool.memset(ident[:, :], 0.0).then_inc(consts, 1)
            pool.wait_ge(consts, 1)
            pool.affine_select(out=ident[:, :], in_=ident[:, :], compare_op=ALU.not_equal, fill=1.0,
                               base=0, pattern=[[-1, P]], channel_multiplier=1).then_inc(consts, 1)

        @block.tensor
        def _(pe):
            pe.wait_ge(weights, 64)
            pe.wait_ge(consts, 2)
            with pe.Fori(0, groups) as g:
                def up(e):
                    for c in range(HK):
                        n = e * HK + c
                        if n >= 4:
                            pe.wait_ge(hid_ready, g * (E * HK) + n - 3)
                        pe.matmul(b_z[n % 4][:, :], w1[:, e, P * c:P * c + P],
                                  flat(xt_keep[:, bass.ds(g * TB, TB), :]), start=True, stop=True)\
                            .then_inc(z_done, 1)

                def down(e):
                    pe.wait_ge(hid_ready, g * (E * HK) + (e + 1) * HK)
                    if e >= 2:
                        pe.wait_ge(y_added, g * E + e - 1)
                    for j in range(TB):
                        for c in range(HK):
                            mm = pe.matmul(b_y[e % 2][:, P * j:P * j + P], hid[e % 2][:, c, P * j:P * j + P],
                                           w2[:, e * HK + c, :], start=(c == 0), stop=(c == HK - 1))
                    mm.then_inc(y_done, 1)

                up(0)
                pe.wait_ge(gate_ready, g + 1)
                for j in range(TB):
                    mm = pe.transpose(b_g[0:E, P * j:P * j + P], gate[:, j, :], ident[:, :])
                mm.then_inc(gate_turned, 1)
                up(1)
                pe.wait_ge(gate_t_ready, g + 1)
                for j in range(TB):
                    mm = pe.matmul(b_b[:, P * j:P * j + P], gate_t[:, P * j:P * j + P], b2r[:, :],
                                   start=True, stop=True)
                mm.then_inc(bias_done, 1)
                for e in range(E):
                    if e + 2 < E:
                        down(e)
                        up(e + 2)
                    else:
                        down(e)

        @block.scalar
        def _(act):
            act.wait_ge(weights, 64)
            if softmax_gates:
                act.wait_ge(shifted, 1)
                act.activation(gates[:, :, 0:E], gates[:, :, 0:E], ACT.Exp).then_inc(exped, 1)
            with act.Fori(0, groups) as g:
                for e in range(E):
                    for c in range(HK):
                        n = e * HK + c
                        act.wait_ge(z_done, g * (E * HK) + n + 1)
                        if e >= 2:
                            act.wait_ge(y_done, g * E + e - 1)
                        act.activation(hid[e % 2][:, c, :], b_z[n % 4][:, :], ACT.Gelu,
                                       bias=b1c[:, n:n + 1]).then_inc(hid_ready, 1)

        @block.vector
        def _(v):
            me = Done(v, own)
            if softmax_gates:
                with Scope(nc, tag + "_gates") as t:
                    best = t.sb("best", [P, tiles])
                    best2 = t.sb("best2", [P, tiles])
                    pick = [t.sb(f"pick{k}", [P, tiles, E]) for k in range(2)]
                    work = t.sb("work", [P, tiles, 2])
                T3 = [P, tiles, E]
                gl = gates[:, :, 0:E]
                me.link(v.tensor_reduce(best[:, :], gl, AX.X, ALU.max))
                v.tensor_tensor(gl, gl, over(best[:, :].unsqueeze(2), T3), ALU.subtract).then_inc(shifted, 1)
                v.wait_ge(exped, 1)
                me.link(v.tensor_reduce(best[:, :], gl, AX.X, ALU.add))
                me.link(v.reciprocal(best[:, :], best[:, :]))
                me.link(v.tensor_tensor(gl, gl, over(best[:, :].unsqueeze(2), T3), ALU.mult))
                top_two(v, me, gates, pick, best, best2, work)
                me.link(v.tensor_tensor(pick[0][:, :, :], pick[0][:, :, :], pick[1][:, :, :], ALU.add))
                me.link(v.tensor_tensor(gl, gl, pick[0][:, :, :], ALU.mult))
            first = me.n
            per = 1 + (TB - 1) * (E - 1)
            with v.Fori(0, groups) as g:
                me.base, me.n = first + per * g, 0
                xs = x_keep[:, bass.ds(g * TB, TB), :]
                v.tensor_copy(gate[:, :, :], gates[:, bass.ds(g * TB, TB), 0:E]).then_inc(gate_ready, 1)
                v.wait_ge(gate_turned, g + 1)
                v.tensor_copy(gate_t[:, :], b_g[0:E, :]).then_inc(gate_t_ready, 1)
                v.wait_ge(bias_done, g + 1)
                me.link(v.tensor_tensor(acc[:, :, :], xs, b_b[:, :].rearrange("p (a b) -> p a b", a=TB), ALU.add))
                for e in range(E):
                    v.wait_ge(y_done, g * E + e + 1)
                    for j in range(TB):
                        ins = v.scalar_tensor_tensor(out=acc[:, j, :] if e < E - 1 else xs[:, j, :],
                                                     in0=b_y[e % 2][:, P * j:P * j + P], scalar=gate[:, j, e:e + 1],
                                                     in1=acc[:, j, :], op0=ALU.mult, op1=ALU.add)
                        if e < E - 1 and j < TB - 1:
                            me.mark(ins)
                    if e < E - 1:
                        ins.then_inc(y_added, 1)
                        me.wait()
                        v.wait_ge(y_added, g * E + e + 1)
                    else:
                        ins.then_inc(y_added, 1)
                        v.wait_ge(y_added, g * E + e + 1)
                        v.sem_inc(turn, 1)


def network(nc, t, out):
    x, adj = t["x"], t["adj"]
    tiles = x.shape[0]
    nodes = tiles * P
    n_edges = t["L0_ffn_edge_index"].shape[1]
    gmax = n_edges // GROUP + tiles + SPARE
    sorted_edges = nc.dram_tensor("sorted_edges", (gmax * GROUP, 1), I32).ap()
    table = nc.dram_tensor("node_table", (nodes, ROW), F32).ap()
    with Scope(nc, "keep") as s:
        keep = {"groups": s.sb("groups", [P, gmax + 2], I32)}
        keep["hub"] = s.sb("hub", [P, tiles])
        keep["gates"] = s.sb("gates", [P, tiles, CH])
        turns = n_edges // (P * 2 * CHUNKS)
        late = [s.sb(name, [P, (turns - EARLY) * 2 * CHUNKS], I32) for name in ("late_slots", "late_values")]
        sort_edges(nc, t["L0_ffn_edge_index"], sorted_edges, keep["groups"], keep["hub"], late, nodes)
        keep["x"] = s.sb("x", [P, tiles, P])
        keep["xt"] = s.sb("xt", [P, tiles, P])
        with Scope(nc, "edge") as m:
            keep["h"] = m.sb("h", [P, tiles, ROW])
            gin_layer(nc, x, adj, {
                "W1": t["L0_gnn_W1"], "b1": t["L0_gnn_b1"], "rms": t["L0_gnn_rms_weight"],
                "W2": t["L0_gnn_W2"], "b2": t["L0_gnn_b2"], "eps": t["L0_gnn_epsilon"],
                "W_gat": t["L0_ffn_W_gat"]}, keep, late, sorted_edges)
            keep["dst"] = m.sb("dst", [P, tiles, 2 * HEADS])
            keep["acc"] = m.sb("acc", [P, tiles, ROW])
            edge_attention(nc, {
                "att_src": t["L0_ffn_att_src"].rearrange("h c -> (h c)"),
                "att_dst": t["L0_ffn_att_dst"].rearrange("h c -> (h c)"),
                "b_gat": t["L0_ffn_b_gat"], "ln_gamma": t["L0_ffn_ln_gamma"],
                "ln_beta": t["L0_ffn_ln_beta"]}, sorted_edges, table, keep)
        experts(nc, "moe0", {"W1": t["L0_ffn_W1"], "b1": t["L0_ffn_b1"], "W2": t["L0_ffn_W2"],
                             "b2": t["L0_ffn_b2"]}, keep, False, None)
        keep["logits"] = s.sb("logits", [P, tiles, t["L1_ffn_gate_w"].shape[1]])
        dense_attention(nc, adj, {"W": t["L1_gnn_W"], "a": t["L1_gnn_a"], "gate_w": t["L1_ffn_gate_w"],
                                  "gate_b": t["L1_ffn_gate_b"]}, keep)
        experts(nc, "moe1", {"W1": t["L1_ffn_W1"], "b1": t["L1_ffn_b1"], "W2": t["L1_ffn_W2"],
                             "b2": t["L1_ffn_b2"]}, dict(keep, gates=keep["logits"]), True, out)


_INS = ["x", "adj", "L0_gnn_epsilon", "L0_gnn_W1", "L0_gnn_b1", "L0_gnn_rms_weight", "L0_gnn_W2", "L0_gnn_b2",
        "L0_ffn_W_gat", "L0_ffn_att_src", "L0_ffn_att_dst", "L0_ffn_b_gat", "L0_ffn_ln_gamma", "L0_ffn_ln_beta",
        "L0_ffn_W1", "L0_ffn_b1", "L0_ffn_W2", "L0_ffn_b2", "L0_ffn_edge_index", "L1_gnn_W", "L1_gnn_a",
        "L1_ffn_gate_w", "L1_ffn_gate_b", "L1_ffn_W1", "L1_ffn_b1", "L1_ffn_W2", "L1_ffn_b2"]


def kernel(**inputs):
    import numpy as _np
    import concourse.bacc as _bacc
    from concourse import mybir as _mybir
    from concourse.bass_utils import run_bass_kernel_spmd as _run

    nc = _bacc.Bacc("TRN2", target_bir_lowering=False, num_devices=1)
    arrays, args = {}, {}
    for name in _INS:
        a = _np.ascontiguousarray(inputs[name])
        if a.ndim == 0:
            a = a.reshape(1)
        arrays[f"in_{name}"] = a
        args[name] = nc.dram_tensor(f"in_{name}", a.shape, _mybir.dt.from_np(a.dtype), kind="ExternalInput").ap()
    shape = _np.shape(inputs["x"])
    out = nc.dram_tensor("out_0", shape, _mybir.dt.float32, kind="ExternalOutput").ap()
    network(nc, args, out)
    r = _run(nc, [arrays], core_ids=[0])
    return r.results[0]["out_0"]
```
